# Optimizing a Trainium2 kernel written in Bass

```python
import numpy as np
import jax
import jax.numpy as jnp

def _softmax(x, axis=-1):
    return jax.nn.softmax(x, axis=axis)

def _gelu(x):
    return jax.nn.gelu(x, approximate=True)

def _silu(x):
    return jax.nn.silu(x)

def _sigmoid(x):
    return jax.nn.sigmoid(x)

def _layernorm(x, axis=-1, eps=1e-05):
    m = jnp.mean(x, axis=axis, keepdims=True)
    v = jnp.var(x, axis=axis, keepdims=True)
    return (x - m) / jnp.sqrt(v + eps)

def _scatter_add(tgt, idx, src, axis=0):
    return tgt.at[idx].add(src)

def _segment_sum(src, seg, n):
    return jax.ops.segment_sum(src, seg, n)
kernel_name = 'mk_seq_postln_d2_jaxref_r8_c7d769'

def setup_inputs(seed: int=0):
    np.random.seed(seed)
    _w = jnp.asarray

    def _L0_attn_setup():
        import jax, jax.numpy as jnp
        import numpy as np
        import math
        H = 128
        S = 16
        K = 4
        INNER = 2 * H
        BATCH, L = (2, 512)

        def _linrec_combine(c1, c2):
            a1, b1 = c1
            a2, b2 = c2
            return (a1 * a2, a2 * b1 + b2)
        key = jax.random.key(seed)
        ks = jax.random.split(key, 8)
        x = jax.random.normal(ks[0], (BATCH, L, H), dtype=jnp.float32)
        W_in = jax.random.normal(ks[1], (2 * INNER, H), dtype=jnp.float32) * 0.02
        conv_w = jax.random.normal(ks[2], (INNER, 1, K), dtype=jnp.float32) * 0.1
        conv_b = jnp.zeros((INNER,), dtype=jnp.float32)
        W_x = jax.random.normal(ks[3], (2 * S + INNER, INNER), dtype=jnp.float32) * 0.02
        W_dt = jax.random.normal(ks[4], (INNER, INNER), dtype=jnp.float32) * 0.02
        u = jax.random.uniform(ks[5], (INNER,), dtype=jnp.float32)
        b_dt = jnp.exp(u * (math.log(0.1) - math.log(0.001)) + math.log(0.001))
        A_log = jnp.log(jnp.broadcast_to(jnp.arange(1, S + 1, dtype=jnp.float32), (INNER, S)))
        D = jnp.ones((INNER,), dtype=jnp.float32)
        W_out = jax.random.normal(ks[6], (H, INNER), dtype=jnp.float32) * 0.02
        return {'x': x, 'W_in': W_in, 'conv_w': conv_w, 'conv_b': conv_b, 'W_x': W_x, 'W_dt': W_dt, 'b_dt': b_dt, 'A_log': A_log, 'D': D, 'W_out': W_out}
    _L0_attn_in = _L0_attn_setup()

    def _L0_ffn_setup():
        import jax, jax.numpy as jnp
        import numpy as np
        FP8_MAX = 448.0
        key = jax.random.key(seed)
        k_x, k_w, k_b = jax.random.split(key, 3)
        B, S, IN, OUT = (4, 1024, 128, 128)
        x = jax.random.normal(k_x, (B, S, IN), dtype=jnp.float32)
        w_fp32 = jax.random.normal(k_w, (OUT, IN), dtype=jnp.float32)
        weight_fp8 = w_fp32.astype(jnp.float8_e4m3fn).astype(jnp.float32)
        bias = jax.random.normal(k_b, (OUT,), dtype=jnp.float32)
        input_scale = jnp.ones((1,), dtype=jnp.float32)
        weight_scale = jnp.ones((1,), dtype=jnp.float32)
        return {'x': x, 'weight_fp8': weight_fp8, 'bias': bias, 'input_scale': input_scale, 'weight_scale': weight_scale}
    _L0_ffn_in = _L0_ffn_setup()

    def _L1_attn_setup():
        import jax, jax.numpy as jnp
        import numpy as np
        S, B, E = (256, 8, 128)
        GAMMA = 0.5
        key = jax.random.key(seed)
        ks = jax.random.split(key, 4)
        w_scale = 1.0 / E
        inputs = jax.random.normal(ks[0], (S, B, E), dtype=jnp.float32)
        Wq = jax.random.normal(ks[1], (E, E), dtype=jnp.float32) * w_scale
        Wk = jax.random.normal(ks[2], (E, E), dtype=jnp.float32) * w_scale
        Wv = jax.random.normal(ks[3], (E, E), dtype=jnp.float32) * w_scale
        bq = jnp.zeros((E,), jnp.float32)
        bk = jnp.zeros((E,), jnp.float32)
        bv = jnp.zeros((E,), jnp.float32)
        return {'inputs': inputs, 'Wq': Wq, 'bq': bq, 'Wk': Wk, 'bk': bk, 'Wv': Wv, 'bv': bv}
    _L1_attn_in = _L1_attn_setup()

    def _L1_ffn_setup():
        import jax, jax.numpy as jnp
        import numpy as np
        DIM = 128

        def _reference_tuple_inner(x, W_r, W_k, W_v, mu_r, mu_k):
            B, T, C = x.shape
            x_prev = jnp.concatenate([jnp.zeros((B, 1, C), x.dtype), x[:, :-1, :]], axis=1)
            xr = mu_r * x + (1.0 - mu_r) * x_prev
            xk = mu_k * x + (1.0 - mu_k) * x_prev
            r = jax.nn.sigmoid(jnp.einsum('btc,dc->btd', xr, W_r))
            k = jnp.einsum('btc,dc->btd', xk, W_k)
            k_act = jnp.square(jax.nn.relu(k))
            out = r * jnp.einsum('btc,dc->btd', k_act, W_v)
            new_state = x[:, -1, :]
            return (out, new_state)
        key = jax.random.key(seed)
        ks = jax.random.split(key, 6)
        B, T, C = (8, 256, DIM)
        x = jax.random.normal(ks[0], (B, T, C), dtype=jnp.float32)
        s = 1.0 / np.sqrt(C)
        W_r = jax.random.uniform(ks[1], (C, C), jnp.float32, -s, s)
        W_k = jax.random.uniform(ks[2], (C, C), jnp.float32, -s, s)
        W_v = jax.random.uniform(ks[3], (C, C), jnp.float32, -s, s)
        mu_r = jax.random.uniform(ks[4], (C,), jnp.float32)
        mu_k = jax.random.uniform(ks[5], (C,), jnp.float32)
        return {'x': x, 'W_r': W_r, 'W_k': W_k, 'W_v': W_v, 'mu_r': mu_r, 'mu_k': mu_k}
    _L1_ffn_in = _L1_ffn_setup()
    _d = {'L0_attn_x': _L0_attn_in['x'], 'L0_attn_W_in': _L0_attn_in['W_in'], 'L0_attn_conv_w': _L0_attn_in['conv_w'], 'L0_attn_conv_b': _L0_attn_in['conv_b'], 'L0_attn_W_x': _L0_attn_in['W_x'], 'L0_attn_W_dt': _L0_attn_in['W_dt'], 'L0_attn_b_dt': _L0_attn_in['b_dt'], 'L0_attn_A_log': _L0_attn_in['A_log'], 'L0_attn_D': _L0_attn_in['D'], 'L0_attn_W_out': _L0_attn_in['W_out'], 'L0_ffn_weight_fp8': _L0_ffn_in['weight_fp8'], 'L0_ffn_bias': _L0_ffn_in['bias'], 'L0_ffn_input_scale': _L0_ffn_in['input_scale'], 'L0_ffn_weight_scale': _L0_ffn_in['weight_scale'], 'L1_attn_Wq': _L1_attn_in['Wq'], 'L1_attn_bq': _L1_attn_in['bq'], 'L1_attn_Wk': _L1_attn_in['Wk'], 'L1_attn_bk': _L1_attn_in['bk'], 'L1_attn_Wv': _L1_attn_in['Wv'], 'L1_attn_bv': _L1_attn_in['bv'], 'L1_ffn_W_r': _L1_ffn_in['W_r'], 'L1_ffn_W_k': _L1_ffn_in['W_k'], 'L1_ffn_W_v': _L1_ffn_in['W_v'], 'L1_ffn_mu_r': _L1_ffn_in['mu_r'], 'L1_ffn_mu_k': _L1_ffn_in['mu_k']}
    _x0 = _d['L0_attn_x']
    _d['L0_attn_x'] = jax.random.normal(jax.random.fold_in(jax.random.key(seed), 1), (8, 512, 128), dtype=_x0.dtype)
    del _x0
    return _d

def reference(L0_attn_x, L0_attn_W_in, L0_attn_conv_w, L0_attn_conv_b, L0_attn_W_x, L0_attn_W_dt, L0_attn_b_dt, L0_attn_A_log, L0_attn_D, L0_attn_W_out, L0_ffn_weight_fp8, L0_ffn_bias, L0_ffn_input_scale, L0_ffn_weight_scale, L1_attn_Wq, L1_attn_bq, L1_attn_Wk, L1_attn_bk, L1_attn_Wv, L1_attn_bv, L1_ffn_W_r, L1_ffn_W_k, L1_ffn_W_v, L1_ffn_mu_r, L1_ffn_mu_k):

    def _L0_attn_ref(x, W_in, conv_w, conv_b, W_x, W_dt, b_dt, A_log, D, W_out):
        import jax, jax.numpy as jnp
        import numpy as np
        import math
        H = 128
        S = 16
        K = 4
        INNER = 2 * H
        BATCH, L = (2, 512)

        def _linrec_combine(c1, c2):
            a1, b1 = c1
            a2, b2 = c2
            return (a1 * a2, a2 * b1 + b2)
        xz = jnp.einsum('blh,ih->bli', x, W_in)
        x_proj, z = jnp.split(xz, 2, axis=-1)
        xc = jnp.transpose(x_proj, (0, 2, 1))
        xc = jax.lax.conv_general_dilated(xc, conv_w, window_strides=(1,), padding=[(K - 1, 0)], dimension_numbers=('NCH', 'OIH', 'NCH'), feature_group_count=INNER)
        xc = xc + conv_b[None, :, None]
        x_conv = jax.nn.silu(jnp.transpose(xc, (0, 2, 1)))
        x_ssm = jnp.einsum('bli,oi->blo', x_conv, W_x)
        Bm = x_ssm[..., :S]
        Cm = x_ssm[..., S:2 * S]
        dt_in = x_ssm[..., 2 * S:]
        dt = jax.nn.softplus(jnp.einsum('bli,oi->blo', dt_in, W_dt) + b_dt)
        alpha = jax.nn.sigmoid(dt * 0.1)
        B_gate = jax.nn.sigmoid(jnp.mean(Bm, axis=-1, keepdims=True))
        gated = (1.0 - alpha) * B_gate * x_conv
        alpha_c = jnp.clip(alpha, 0.01, 0.99)
        _, h = jax.lax.associative_scan(_linrec_combine, (alpha_c, gated), axis=1)
        C_gate = jax.nn.sigmoid(jnp.mean(Cm, axis=-1, keepdims=True))
        y = h * C_gate + D * x_conv
        y = y * jax.nn.silu(z)
        out = jnp.einsum('bli,hi->blh', y, W_out)
        return out

    def _L0_ffn_ref(x, weight_fp8, bias, input_scale, weight_scale):
        import jax, jax.numpy as jnp
        import numpy as np
        FP8_MAX = 448.0
        x_q = jnp.clip(x / input_scale, -FP8_MAX, FP8_MAX)
        x_dq = x_q.astype(jnp.float8_e4m3fn).astype(x.dtype) * input_scale
        w_dq = weight_fp8 * weight_scale
        out = jnp.einsum('bsi,oi->bso', x_dq, w_dq) + bias
        return out

    def _L1_attn_ref(inputs, Wq, bq, Wk, bk, Wv, bv):
        import jax, jax.numpy as jnp
        import numpy as np
        S, B, E = (256, 8, 128)
        GAMMA = 0.5
        q = inputs @ Wq.T + bq
        k = inputs @ Wk.T + bk
        v = inputs @ Wv.T + bv
        q2 = jnp.sum(q * q, axis=-1)
        k2 = jnp.sum(k * k, axis=-1)
        qk = jnp.einsum('tbe,jbe->tjb', q, k)
        d2 = q2[:, None, :] + k2[None, :, :] - 2.0 * qk
        d2 = jnp.maximum(d2, 0.0)
        sim = jax.nn.softmax(-GAMMA * d2, axis=1)
        return jnp.einsum('tjb,jbe->tbe', sim, v)

    def _L1_ffn_ref(x, W_r, W_k, W_v, mu_r, mu_k):
        import jax, jax.numpy as jnp
        import numpy as np
        DIM = 128

        def _reference_tuple_inner(x, W_r, W_k, W_v, mu_r, mu_k):
            B, T, C = x.shape
            x_prev = jnp.concatenate([jnp.zeros((B, 1, C), x.dtype), x[:, :-1, :]], axis=1)
            xr = mu_r * x + (1.0 - mu_r) * x_prev
            xk = mu_k * x + (1.0 - mu_k) * x_prev
            r = jax.nn.sigmoid(jnp.einsum('btc,dc->btd', xr, W_r))
            k = jnp.einsum('btc,dc->btd', xk, W_k)
            k_act = jnp.square(jax.nn.relu(k))
            out = r * jnp.einsum('btc,dc->btd', k_act, W_v)
            new_state = x[:, -1, :]
            return (out, new_state)
        return _reference_tuple_inner(x, W_r, W_k, W_v, mu_r, mu_k)[0]
    x = L0_attn_x
    x = _layernorm(x + _L0_attn_ref(x, L0_attn_W_in, L0_attn_conv_w, L0_attn_conv_b, L0_attn_W_x, L0_attn_W_dt, L0_attn_b_dt, L0_attn_A_log, L0_attn_D, L0_attn_W_out), axis=-1)
    x = _layernorm(x + _L0_ffn_ref(x, L0_ffn_weight_fp8, L0_ffn_bias, L0_ffn_input_scale, L0_ffn_weight_scale), axis=-1)
    x = _layernorm(x + _L1_attn_ref(x, L1_attn_Wq, L1_attn_bq, L1_attn_Wk, L1_attn_bk, L1_attn_Wv, L1_attn_bv), axis=-1)
    x = _layernorm(x + _L1_ffn_ref(x, L1_ffn_W_r, L1_ffn_W_k, L1_ffn_W_v, L1_ffn_mu_r, L1_ffn_mu_k), axis=-1)
    return x

_drawn_inputs = setup_inputs


def setup_inputs(seed=0):
    import zlib

    import numpy as np

    out = dict(_drawn_inputs(seed))
    spreads = {'L0_attn_conv_b': (0.0, 0.687),
     'L0_attn_D': (1.0, 0.6),
     'L1_attn_bq': (0.0, 0.8),
     'L1_attn_bk': (0.0, 0.8),
     'L1_attn_bv': (0.0, 0.1)}
    factors = {'L0_attn_W_in': 5.603,
     'L0_attn_conv_w': 8.0,
     'L0_attn_W_x': 8.0,
     'L0_attn_W_dt': 8.0,
     'L0_attn_b_dt': 200.0,
     'L0_attn_W_out': 5.486,
     'L1_attn_Wq': 8.0,
     'L1_attn_Wk': 8.0,
     'L1_ffn_W_r': 3.109,
     'L1_ffn_mu_r': 6.262}
    for name, (base, spread) in spreads.items():
        noise = np.random.default_rng([zlib.crc32(name.encode()), seed]).standard_normal(out[name].shape)
        drawn = base * np.exp(spread * noise) if base else spread * noise
        out[name] = jnp.asarray(drawn.astype(out[name].dtype))
    for name, factor in factors.items():
        out[name] = (out[name] * factor).astype(out[name].dtype)
    return out
```

```python
from contextlib import ExitStack

import concourse.bass as bass
from concourse import mybir

ALU = mybir.AluOpType
ACT = mybir.ActivationFunctionType
AXIS_X = mybir.AxisListType.X
F32 = mybir.dt.float32
BF16 = mybir.dt.bfloat16
I32 = mybir.dt.int32

P = 128
SEQS, LENGTH, CHANNELS = 8, 512, 128
TOKENS = SEQS * LENGTH
HALVES = 2
INNER = HALVES * P
TAPS = 4
STATE = 16
CHUNK = 512
SPAN = CHUNK // SEQS
GROUP = P // SEQS
GROUPS = CHUNK // P
CHUNKS = TOKENS // CHUNK
EPS = 1e-5
FP8_MAX = 448.0
SOFTPLUS_KNEE = 20.0
MASKED = -1e30

W_COMB_X = 0
W_COMB_DT = W_COMB_X + HALVES * INNER
W_CENTRED = W_COMB_DT + HALVES * INNER
W_Q = W_CENTRED + 4 * P
W_K = W_Q + P
W_FR = W_K + P
W_FK = W_FR + P
W_FV = W_FK + P
W_COLS = W_FV + P
V_CONV_W = 0
V_CONV_B = V_CONV_W + HALVES * TAPS
V_B_DT = V_CONV_B + HALVES
V_D = V_B_DT + HALVES
V_BIAS8 = V_D + HALVES
V_BV = V_BIAS8 + 1
V_BQ = V_BV + 1
V_BK = V_BQ + 1
V_MU_R = V_BK + 1
V_MU_K = V_MU_R + 1
V_COLS = V_MU_K + 1
C_IDENT = 0
C_CENTRE = P
C_MASK = 2 * P
C_COLS = 3 * P


def build(nc, x_t, w_in_t, vectors, weights, gate_rows, scales, constants, out_t):
    with ExitStack() as ctx:
        def sb(name, shape, dt=F32):
            return ctx.enter_context(nc.sbuf_tensor(name, shape, dt))

        def sem(name):
            return ctx.enter_context(nc.semaphore(name))

        xT = sb("xT", [P, TOKENS])
        xconv = sb("xconv", [P, HALVES, TOKENS])
        silu_z = sb("silu_z", [P, HALVES, TOKENS])
        decay = sb("decay", [P, HALVES, TOKENS])
        x3 = sb("x3", [P, SEQS, LENGTH + 1])
        tmp = sb("tmp", [P, 16, CHUNK])

        w_in = sb("w_in", [P, 2 * INNER])
        vec = sb("vec", [P, V_COLS])
        w = sb("w", [P, W_COLS])
        gate_w = sb("gate_w", [STATE, 2, INNER])
        sc = sb("sc", [P, 2])
        const = sb("const", [P, C_COLS])
        comb = sb("comb", [P, HALVES, INNER])
        gates = sb("gates", [P, 2, HALVES, P])
        w8 = sb("w8", [P, 3, P], BF16)
        w8_rest = sb("w8_rest", [P, P])
        sixteenth = sb("sixteenth", [STATE, P])
        mean_w = sb("mean_w", [P, P])
        minus_half = sb("minus_half", [P, P])
        row_sum = sb("row_sum", [P, 4])
        both_scales = sb("both_scales", [P, 1])
        inv_scale = sb("inv_scale", [P, 1])
        knee = sb("knee", [P, HALVES])
        alpha_bias = sb("alpha_bias", [P, HALVES])
        one_minus_mu = sb("one_minus_mu", [P, 2])
        centred_bias = sb("centred_bias", [P, 2])
        eps = sb("eps", [P, 1])
        credit = sb("credit", [P, 32])
        neg_max = sb("neg_max", [P, 4, GROUPS])
        exp_sum = sb("exp_sum", [P, 4, GROUPS])
        inv_sum = sb("inv_sum", [P, 4, GROUPS])
        quant = sb("quant", [P, 4, CHUNK], BF16)

        ident = const[:, C_IDENT:C_IDENT + P]
        centre = const[:, C_CENTRE:C_CENTRE + P]
        mask = const[:, C_MASK:C_MASK + P]
        mask_all_groups = mask.unsqueeze(1).broadcast_to([P, GROUPS, P])

        y_chunks = xconv[:, :, :].rearrange("p h (b c g l) -> p h c g b l", b=SEQS, c=CHUNKS, g=GROUPS)
        xT_chunks = xT[:, :].rearrange("p (b c g l) -> p c g b l", b=SEQS, c=CHUNKS, g=GROUPS)
        x3_chunks = x3[:, :, 1:].rearrange("p b (c g l) -> p c g b l", c=CHUNKS, g=GROUPS)
        four_a = decay[:, :, :].rearrange("p h (k n) -> p (h k) n", n=CHUNK)
        four_b = silu_z[:, :, :].rearrange("p h (k n) -> p (h k) n", n=CHUNK)
        x1, xs, step8, sq = (four_a[:, 4 * n:4 * n + 4] for n in range(4))
        x2, q, k_, q_sq = (four_b[:, 4 * n:4 * n + 4] for n in range(4))
        k_sq, v = xs, step8
        rstd, prob, prob_t, y3 = (tmp[:, 4 * n:4 * n + 4] for n in range(4))

        psum = ctx.enter_context(nc.psum_tensor("psum", [P, 8, CHUNK], F32))
        bank = [psum[:, n, :] for n in range(8)]

        def grouped(ap):
            return ap.rearrange("p (g n) -> p g n", g=GROUPS)

        def by_position(ap):
            return ap.rearrange("p (g b l) -> p g b l", g=GROUPS, b=SEQS)

        x_first, x_rest, small_in, weights_in = sem("x_first"), sem("x_rest"), sem("small_in"), sem("weights_in")
        filled = sem("filled")
        xp_ready, z_ready = sem("xp_ready"), sem("z_ready")
        tap_done, conv_done = sem("tap_done"), sem("conv_done")
        conv_step = sem("conv_step")
        xconv_done, z_done = sem("xconv_done"), sem("z_done")
        prep_mm, prep = sem("prep_mm"), sem("prep")
        dt_ready, dt_capped, dt_exp, dt_ln, dt_sum = (sem(n) for n in ("dt_ready", "dt_capped", "dt_exp", "dt_ln", "dt_sum"))
        gate_ready, gate_done, alpha_done = sem("gate_ready"), sem("gate_done"), sem("alpha_done")
        scan_step, y_done = sem("scan_step"), sem("y_done")
        out_ready, sq_done, var_ready, var_read, rstd_done = (sem(n) for n in ("out_ready", "sq_done", "var_ready", "var_read", "rstd_done"))
        x1_done, xs_done, quant_step, quant_done = (sem(n) for n in ("x1_done", "xs_done", "quant_step", "quant_done"))
        ffn_ready, y2_done, x2_done = sem("ffn_ready"), sem("y2_done"), sem("x2_done")
        q_ready, k_ready, v_ready = sem("q_ready"), sem("k_ready"), sem("v_ready")
        q_done, k_done, v_done = sem("q_done"), sem("k_done"), sem("v_done")
        score_ready, logit_done, max_step, neg_max_done = (sem(n) for n in ("score_ready", "logit_done", "max_step", "neg_max_done"))
        exp_done, inv_done, prob_done = sem("exp_done"), sem("inv_done"), sem("prob_done")
        turned_ready, turned_done = sem("turned_ready"), sem("turned_done")
        att_ready, y3_done, x3_done = sem("att_ready"), sem("y3_done"), sem("x3_done")
        shift_done, xr_done, xk_done = sem("shift_done"), sem("xr_done"), sem("xk_done")
        r_ready, fk_ready, r_done, relu_done, kact_done = (sem(n) for n in ("r_ready", "fk_ready", "r_done", "relu_done", "kact_done"))
        fv_ready, rv_done, sum_done, cen_ready, cen_done = (sem(n) for n in ("fv_ready", "rv_done", "sum_done", "cen_ready", "cen_done"))
        last_sq, last_var, last_ln, last_rstd, last_out, stored = (
            sem(n) for n in ("last_sq", "last_var", "last_ln", "last_rstd", "last_out", "stored"))

        CONV0, Z0, XC0, X3_0, DT0, GATE0, Y0, VAR0, TURN0, LOGIT0, Y3_0, SMALL0 = 4, 4, 4, 4, 4, 4, 4, 2, 4, 4, 4, 2

        block = ctx.enter_context(nc.Block())

        @block.sync
        def _(sp):
            half_x = 2 * CHUNK
            sp.dma_start(w_in[:, :], w_in_t).then_inc(small_in, 16)
            sp.dma_start(xT[:, 0:half_x], x_t[:, 0:half_x]).then_inc(x_first, 16)
            sp.dma_start(vec[:, :], vectors).then_inc(small_in, 16)
            sp.dma_start(xT[:, half_x:], x_t[:, half_x:]).then_inc(x_rest, 16)
            with sp.Fori(0, SEQS // 2) as i:
                for k in range(2):
                    b = i * 2 + k
                    sp.wait_ge(last_out, b + 1 + SMALL0)
                    sp.dma_start(out_t[:, bass.ts(b, CHUNK)], decay[:, 0, bass.ts(b, CHUNK)]).then_inc(stored, 16)
            sp.wait_ge(stored, 16 * SEQS)

        @block.gpsimd
        def _(pool):
            pool.wait_ge(filled, 1)

        @block.tensor
        def _(pe):
            def mm(out, lhs_t, rhs, first=True, last=True):
                return nc.tensor.matmul(out, lhs_t, rhs, start=first, stop=last)

            pe.wait_ge(small_in, 32)
            pe.wait_ge(x_first, 16)
            pe.wait_ge(filled, 1)
            with pe.Fori(0, SEQS // 2) as i:
                for k in range(4):
                    j = i * 4 + k
                    b = i * 2 + k // 2
                    if k == 2:
                        pe.wait_ge(x_rest, 16)
                    pe.wait_ge(conv_done, j + 1)
                    mm(bank[k], w_in[:, (k % 2) * P:(k % 2 + 1) * P], xT[:, bass.ts(b, CHUNK)]).then_inc(xp_ready, 1)
                    pe.wait_ge(z_done, j + 1)
                    mm(bank[4 + k], w_in[:, INNER + (k % 2) * P:INNER + (k % 2 + 1) * P],
                       xT[:, bass.ts(b, CHUNK)]).then_inc(z_ready, 1)

            pe.wait_ge(weights_in, 64)
            pe.wait_ge(z_done, Z0 + 16)
            for ih in range(HALVES):
                for mh in range(HALVES):
                    last = mm(bank[4 + ih][:, 0:INNER],
                              w[:, W_COMB_X + mh * INNER + ih * P:W_COMB_X + mh * INNER + (ih + 1) * P],
                              w[:, W_COMB_DT + mh * INNER:W_COMB_DT + (mh + 1) * INNER], mh == 0, mh == 1)
            last.then_inc(prep_mm, 1)
            for gate in range(2):
                for ih in range(HALVES):
                    last = mm(bank[6][:, (2 * gate + ih) * P:(2 * gate + ih + 1) * P],
                              gate_w[:, gate, ih * P:(ih + 1) * P], sixteenth[:, :])
            last.then_inc(prep_mm, 1)
            mm(bank[7][:, 0:2], centre, vec[:, V_BIAS8:V_BIAS8 + 2]).then_inc(prep_mm, 1)

            pe.wait_ge(prep, 1)
            pe.wait_ge(conv_done, CONV0 + 16)
            with pe.Fori(0, SEQS // 2) as i:
                for k in range(4):
                    j = i * 4 + k
                    b = i * 2 + k // 2
                    pe.wait_ge(xconv_done, XC0 + i * 4 + (k // 2) * 2 + 2)
                    pe.wait_ge(dt_sum, j + 1)
                    for ih in range(HALVES):
                        last = mm(bank[k], comb[:, ih, (k % 2) * P:(k % 2 + 1) * P],
                                  xconv[:, ih, bass.ts(b, CHUNK)], ih == 0, ih == 1)
                    last.then_inc(dt_ready, 1)

            pe.wait_ge(prep, 3)
            with pe.Fori(0, SEQS // 2) as i:
                for k in range(2):
                    b = i * 2 + k
                    pe.wait_ge(gate_done, i * 4 + 2 * k + 2)
                    for gate in range(2):
                        for ih in range(HALVES):
                            last = mm(bank[4 + 2 * k + gate], gates[:, gate, ih, :],
                                      xconv[:, ih, bass.ts(b, CHUNK)], ih == 0, ih == 1)
                        last.then_inc(gate_ready, 1)

            pe.wait_ge(y_done, Y0 + 2 * SEQS)
            pe.wait_ge(gate_done, GATE0 + 2 * SEQS)
            pe.wait_ge(prep, 4)
            with pe.Fori(0, CHUNKS // 4) as i:
                def var(n, k):
                    pe.wait_ge(sq_done, i * 12 + n * 4 + k + 1)
                    pe.wait_ge(var_read, i * 12 + n * 4 + k + 1)
                    mm(bank[4 + k % 2], mean_w[:, :], sq[:, k, :]).then_inc(var_ready, 1)

                for k in range(4):
                    c = i * 4 + k
                    if k < 2:
                        pe.wait_ge(turned_done, i * 4 + k + 3)
                    else:
                        pe.wait_ge(y3_done, i * 4 + k + 1)
                    for ih in range(HALVES):
                        mm(bank[k], w[:, W_CENTRED + ih * P:W_CENTRED + (ih + 1) * P], y_chunks[:, ih, c], ih == 0, False)
                    mm(bank[k], centre, xT_chunks[:, c], False, True).then_inc(out_ready, 1)
                    if k:
                        var(0, k - 1)
                var(0, 3)
                for k in range(4):
                    pe.wait_ge(quant_done, i * 4 + k + 1)
                    if k < 2:
                        pe.wait_ge(logit_done, i * 4 + k + 3)
                    else:
                        pe.wait_ge(y2_done, i * 4 + k - 1)
                    for part in range(3):
                        last = mm(bank[6 + k % 2], w8[:, part, :], quant[:, k, :], part == 0, part == 2)
                    last.then_inc(ffn_ready, 1)
                    if k:
                        var(1, k - 1)
                var(1, 3)
                users = [(x1_done, k) for k in range(4)]
                for k in range(4):
                    pe.wait_ge(x2_done, i * 4 + k + 1)
                    for col, ready, done in ((W_Q, q_ready, q_done), (W_K, k_ready, k_done), (None, v_ready, v_done)):
                        at = len(users) % 4
                        last_user, step = users[-4]
                        pe.wait_ge(last_user, i * 4 + step + 1)
                        if col is not None:
                            last = mm(bank[at], w[:, col:col + P], x2[:, k, :])
                        else:
                            for g in range(GROUPS):
                                last = mm(bank[at][:, g * P:(g + 1) * P], x2[:, k, g * P:(g + 1) * P],
                                          w[:, W_CENTRED + 2 * P:W_CENTRED + 3 * P])
                        last.then_inc(ready, 1)
                        users.append((done, k))
                for k in range(4):
                    s = bank[6 + k % 2]
                    pe.wait_ge(q_done, i * 4 + k + 1)
                    pe.wait_ge(k_done, i * 4 + k + 1)
                    if k < 2:
                        pe.wait_ge(y2_done, i * 4 + k + 3)
                    else:
                        pe.wait_ge(logit_done, LOGIT0 + i * 4 + k - 1)
                    nc.tensor.matmul(s, minus_half[:, :], k_sq[:, k, :], start=True, stop=False, skip_group_check=True)
                    for g in range(GROUPS):
                        cols = slice(g * P, (g + 1) * P)
                        nc.tensor.matmul(s[:, cols], q_sq[:, k, cols], minus_half[:, :], start=False, stop=False, skip_group_check=True)
                        last = nc.tensor.matmul(s[:, cols], q[:, k, cols], k_[:, k, cols], start=False, stop=True, skip_group_check=True)
                    last.then_inc(score_ready, 1)

                def attend(k):
                    pe.wait_ge(turned_done, TURN0 + i * 4 + k + 1)
                    if k < 2:
                        user, step = users[-2 + k]
                        pe.wait_ge(user, i * 4 + step + 1)
                    else:
                        pe.wait_ge(y3_done, Y3_0 + i * 4 + k - 1)
                    for g in range(GROUPS):
                        cols = slice(g * P, (g + 1) * P)
                        last = mm(bank[2 + k % 2][:, cols], v[:, k, cols], prob_t[:, k, cols])
                    last.then_inc(att_ready, 1)

                for k in range(4):
                    pe.wait_ge(prob_done, i * 4 + k + 1)
                    if k < 2:
                        user, step = users[-4 + k]
                        pe.wait_ge(user, i * 4 + step + 1)
                    else:
                        pe.wait_ge(turned_done, TURN0 + i * 4 + k - 1)
                    for g in range(GROUPS):
                        cols = slice(g * P, (g + 1) * P)
                        last = nc.tensor.transpose(bank[k % 2][:, cols], prob[:, k, cols], ident)
                    last.then_inc(turned_ready, 1)
                    if k >= 1:
                        attend(k - 1)
                    if k >= 2:
                        var(2, k - 2)
                attend(3)
                var(2, 2)
                var(2, 3)

            pe.wait_ge(x3_done, X3_0 + CHUNKS)
            with pe.Fori(0, SEQS // 2) as i:
                for k in range(2):
                    b = i * 2 + k
                    pe.wait_ge(xr_done, b + 1)
                    pe.wait_ge(r_done, b + 1)
                    mm(bank[k], w[:, W_FR:W_FR + P], tmp[:, 2 + k, :]).then_inc(r_ready, 1)
                    pe.wait_ge(xk_done, b + 1)
                    pe.wait_ge(relu_done, b + 1)
                    mm(bank[2 + k], w[:, W_FK:W_FK + P], tmp[:, 4 + k, :]).then_inc(fk_ready, 1)
                for k in range(2):
                    b = i * 2 + k
                    pe.wait_ge(kact_done, b + 1)
                    pe.wait_ge(rv_done, b + 1)
                    mm(bank[4 + k], w[:, W_FV:W_FV + P], tmp[:, 10 + k, :]).then_inc(fv_ready, 1)
                for k in range(2):
                    b = i * 2 + k
                    pe.wait_ge(sum_done, b + 1)
                    pe.wait_ge(cen_done, b + 1)
                    mm(bank[6 + k], centre, tmp[:, 12 + k, :]).then_inc(cen_ready, 1)
            pe.wait_ge(r_done, SMALL0 + SEQS)
            with pe.Fori(0, SEQS // 2) as i:
                for k in range(2):
                    b = i * 2 + k
                    pe.wait_ge(last_sq, b + 1)
                    pe.wait_ge(last_ln, b + 1)
                    mm(bank[k], mean_w[:, :], tmp[:, 6 + k, :]).then_inc(last_var, 1)

        @block.scalar
        def _(act):
            act.dma_start(w[:, :], weights).then_inc(weights_in, 16)
            act.dma_start(const[:, :], constants).then_inc(weights_in, 16)
            act.dma_start(gate_w[:, :, :], gate_rows).then_inc(weights_in, 16)
            act.dma_start(sc[:, :], scales.rearrange("(a n) -> a n", a=1).broadcast_to([P, 2])).then_inc(weights_in, 16)

            nc.scalar.preload_act_table(ACT.Silu)
            act.wait_ge(small_in, 32)
            with act.Fori(0, SEQS // 2) as i:
                for k in range(4):
                    j = i * 4 + k
                    h = k % 2
                    act.wait_ge(xp_ready, j + 1)
                    act.wait_ge(xconv_done, j + 1)
                    nc.scalar.activation(tmp[:, k, :], bank[k], ACT.Identity,
                                         bias=vec[:, V_CONV_B + h:V_CONV_B + h + 1],
                                         scale=vec[:, V_CONV_W + h * TAPS + 3:V_CONV_W + h * TAPS + 4]).then_inc(tap_done, 1)
                    act.wait_ge(z_ready, j + 1)
                    nc.scalar.activation(silu_z[:, h, bass.ts(i * 2 + k // 2, CHUNK)], bank[4 + k], ACT.Silu).then_inc(z_done, 1)
                    if k >= 2:
                        act.wait_ge(conv_done, CONV0 + j - 1)
                        nc.scalar.activation(xconv[:, h, bass.ts(i * 2, CHUNK)], tmp[:, k - 2, :], ACT.Silu).then_inc(xconv_done, 1)
                for k in range(2, 4):
                    act.wait_ge(conv_done, CONV0 + i * 4 + k + 1)
                    nc.scalar.activation(xconv[:, k % 2, bass.ts(i * 2 + 1, CHUNK)], tmp[:, k, :], ACT.Silu).then_inc(xconv_done, 1)

            nc.scalar.preload_act_table_set("natural_log_exp_and_others")
            with act.Fori(0, SEQS // 2) as i:
                def ln(k):
                    act.wait_ge(dt_exp, i * 4 + k + 1)
                    nc.scalar.activation(tmp[:, 4 + k, :], tmp[:, 4 + k, :], ACT.Ln, bias=1.0).then_inc(dt_ln, 1)

                for k in range(4):
                    act.wait_ge(dt_capped, i * 4 + k + 1)
                    nc.scalar.activation(tmp[:, 4 + k, :], tmp[:, 4 + k, :], ACT.Exp).then_inc(dt_exp, 1)
                    if k:
                        ln(k - 1)
                ln(3)

            nc.scalar.preload_act_table(ACT.Sigmoid)
            with act.Fori(0, SEQS // 2) as i:
                for k in range(2):
                    for h in range(HALVES):
                        act.wait_ge(dt_sum, DT0 + i * 4 + 2 * k + h + 1)
                        a = decay[:, h, bass.ts(i * 2 + k, CHUNK)]
                        nc.scalar.activation(a, a, ACT.Sigmoid, bias=alpha_bias[:, h:h + 1], scale=0.1).then_inc(alpha_done, 1)
                    for gate in range(2):
                        act.wait_ge(gate_ready, i * 4 + 2 * k + gate + 1)
                        act.wait_ge(y_done, i * 4 + 2 * k + 2)
                        nc.scalar.activation(tmp[:, 2 * k + gate, :], bank[4 + 2 * k + gate], ACT.Sigmoid).then_inc(gate_done, 1)

            nc.scalar.preload_act_table_set("natural_log_exp_and_others")
            with act.Fori(0, CHUNKS // 4) as i:
                def square(n, k, source, ready, at):
                    act.wait_ge(ready, at)
                    nc.scalar.activation(sq[:, k, :], source, ACT.Square).then_inc(sq_done, 1)

                def ln(n, k):
                    act.wait_ge(var_ready, i * 12 + n * 4 + k + 1)
                    act.wait_ge((x3_done, x1_done, x2_done)[n], i * 4 + k + 1)
                    nc.scalar.activation(rstd[:, k, :], bank[4 + k % 2], ACT.Ln, bias=eps[:, 0:1]).then_inc(var_read, 1)

                def exp(n, k):
                    act.wait_ge(var_read, VAR0 + i * 12 + n * 4 + k + 1)
                    nc.scalar.activation(rstd[:, k, :], rstd[:, k, :], ACT.Exp, scale=-0.5).then_inc(rstd_done, 1)

                def scaled(k):
                    act.wait_ge(x1_done, i * 4 + k + 1)
                    nc.scalar.activation(xs[:, k, :], x1[:, k, :], ACT.Identity, scale=inv_scale[:, 0:1]).then_inc(xs_done, 1)

                for k in range(4):
                    square(0, k, bank[k], out_ready, i * 4 + k + 1)
                    if k >= 1:
                        ln(0, k - 1)
                    if k >= 2:
                        scaled(k - 2)
                    if k >= 1:
                        exp(0, k - 1)
                ln(0, 3)
                scaled(2)
                exp(0, 3)
                scaled(3)
                for k in range(4):
                    square(1, k, x2[:, k, :], y2_done, i * 4 + k + 1)
                    if k >= 1:
                        ln(1, k - 1)
                        exp(1, k - 1)
                ln(1, 3)
                exp(1, 3)
                for k in range(4):
                    act.wait_ge(q_ready, i * 4 + k + 1)
                    nc.scalar.activation(q[:, k, :], bank[(4 + 3 * k) % 4], ACT.Identity, bias=vec[:, V_BQ:V_BQ + 1])
                    nc.scalar.activation(q_sq[:, k, :], bank[(4 + 3 * k) % 4], ACT.Square, bias=vec[:, V_BQ:V_BQ + 1]).then_inc(q_done, 1)
                    act.wait_ge(k_ready, i * 4 + k + 1)
                    nc.scalar.activation(k_[:, k, :], bank[(5 + 3 * k) % 4], ACT.Identity, bias=vec[:, V_BK:V_BK + 1])
                    nc.scalar.activation(k_sq[:, k, :], bank[(5 + 3 * k) % 4], ACT.Square, bias=vec[:, V_BK:V_BK + 1]).then_inc(k_done, 1)
                for k in range(4):
                    act.wait_ge(neg_max_done, i * 4 + k + 1)
                    for g in range(GROUPS):
                        cols = slice(g * P, (g + 1) * P)
                        e = nc.scalar.activation(prob[:, k, cols], prob[:, k, cols], ACT.Exp, bias=neg_max[:, k, g:g + 1],
                                                 accum_out=exp_sum[:, k, g:g + 1])
                    e.then_inc(exp_done, 1)

                def turned(k):
                    act.wait_ge(turned_ready, i * 4 + k + 1)
                    nc.scalar.activation(prob_t[:, k, :], bank[k % 2], ACT.Copy).then_inc(turned_done, 1)

                for k in range(4):
                    turned(k)
                    if k >= 1:
                        square(2, k - 1, y3[:, k - 1, :], y3_done, Y3_0 + i * 4 + k)
                    if k >= 2:
                        ln(2, k - 2)
                        exp(2, k - 2)
                square(2, 3, y3[:, 3, :], y3_done, Y3_0 + i * 4 + 4)
                for k in range(2, 4):
                    ln(2, k)
                    exp(2, k)

            nc.scalar.preload_act_table(ACT.Sigmoid)
            with act.Fori(0, SEQS // 2) as i:
                for k in range(2):
                    b = i * 2 + k
                    act.wait_ge(r_ready, b + 1)
                    act.wait_ge(rv_done, b + 1)
                    nc.scalar.activation(tmp[:, 6 + k, :], bank[k], ACT.Sigmoid).then_inc(r_done, 1)
                    act.wait_ge(fk_ready, b + 1)
                    nc.scalar.activation(tmp[:, 8 + k, :], bank[2 + k], ACT.Relu).then_inc(relu_done, 1)
                for k in range(2):
                    b = i * 2 + k
                    act.wait_ge(relu_done, SMALL0 + b + 1)
                    act.wait_ge(rv_done, b + 1)
                    nc.scalar.activation(tmp[:, 10 + k, :], tmp[:, 8 + k, :], ACT.Square).then_inc(kact_done, 1)
                for k in range(2):
                    b = i * 2 + k
                    act.wait_ge(cen_ready, b + 1)
                    nc.scalar.activation(xT[:, bass.ts(b, CHUNK)], bank[6 + k], ACT.Copy).then_inc(cen_done, 1)
            nc.scalar.preload_act_table_set("natural_log_exp_and_others")
            act.wait_ge(rv_done, SMALL0 + SEQS)
            with act.Fori(0, SEQS // 2) as i:
                for k in range(2):
                    b = i * 2 + k
                    act.wait_ge(cen_done, SMALL0 + b + 1)
                    act.wait_ge(last_ln, b + 1)
                    nc.scalar.activation(tmp[:, 6 + k, :], xT[:, bass.ts(b, CHUNK)], ACT.Square).then_inc(last_sq, 1)
                for k in range(2):
                    b = i * 2 + k
                    act.wait_ge(last_var, b + 1)
                    act.wait_ge(last_out, b + 1)
                    nc.scalar.activation(tmp[:, 8 + k, :], bank[k], ACT.Ln, bias=eps[:, 0:1]).then_inc(last_ln, 1)
                for k in range(2):
                    b = i * 2 + k
                    act.wait_ge(last_ln, SMALL0 + b + 1)
                    nc.scalar.activation(tmp[:, 8 + k, :], tmp[:, 8 + k, :], ACT.Exp, scale=-0.5).then_inc(last_rstd, 1)

        @block.vector
        def _(dve):
            tt, ts, stt = nc.vector.tensor_tensor, nc.vector.tensor_scalar, nc.vector.scalar_tensor_tensor

            nc.vector.memset(sixteenth[:, :], 1.0 / STATE)
            nc.vector.memset(mean_w[:, :], 1.0 / CHANNELS)
            nc.vector.memset(minus_half[:, :], -0.5)
            nc.vector.memset(x3[:, :, 0:1], 0.0)
            nc.vector.memset(eps[:, :], EPS).then_inc(filled, 1)
            for at, (ring, n) in enumerate(((conv_done, CONV0), (z_done, Z0), (x3_done, X3_0), (xconv_done, XC0), (dt_sum, DT0), (gate_done, GATE0), (y_done, Y0),
                            (var_read, VAR0), (turned_done, TURN0), (logit_done, LOGIT0), (y3_done, Y3_0),
                            (r_done, SMALL0), (relu_done, SMALL0), (rv_done, SMALL0), (cen_done, SMALL0),
                            (last_ln, SMALL0), (last_out, SMALL0))):
                nc.vector.memset(credit[:, at:at + 1], 0.0).then_inc(ring, n)

            dve.wait_ge(small_in, 32)
            with dve.Fori(0, SEQS // 2) as i:
                for pair in range(2):
                    for tap in (2, 1, 0):
                        shift = TAPS - 1 - tap
                        for h in range(HALVES):
                            k = 2 * pair + h
                            j = i * 4 + k
                            if tap == 2:
                                dve.wait_ge(tap_done, j + 1)
                            else:
                                dve.wait_ge(conv_step, i * 8 + 4 * pair + (2 - tap - 1) * 2 + h + 1)
                            acc = tmp[:, k, shift:]
                            col = V_CONV_W + h * TAPS + tap
                            done = stt(out=acc, in0=bank[k][:, 0:CHUNK - shift], scalar=vec[:, col:col + 1], in1=acc,
                                       op0=ALU.mult, op1=ALU.add)
                            done.then_inc(conv_done if tap == 0 else conv_step, 1)

            step = [0]

            def chain(ins):
                step[0] += 1
                ins.then_inc(prep, 1)

            dve.wait_ge(weights_in, 64)
            dve.wait_ge(prep_mm, 1)
            chain(nc.vector.tensor_copy(comb[:, :, :], psum[:, 4:6, 0:INNER]))
            dve.wait_ge(prep_mm, 2)
            chain(nc.vector.tensor_copy(gates[:, :, :, :], bank[6].rearrange("p (a h n) -> p a h n", a=2, h=2)))
            dve.wait_ge(prep_mm, 3)
            chain(nc.vector.tensor_copy(centred_bias[:, :], bank[7][:, 0:2]))
            ts(knee[:, :], vec[:, V_B_DT:V_B_DT + 2], -1.0, SOFTPLUS_KNEE, ALU.mult, ALU.add)
            ts(alpha_bias[:, :], vec[:, V_B_DT:V_B_DT + 2], -SOFTPLUS_KNEE, 0.1, ALU.add, ALU.mult)
            ts(one_minus_mu[:, :], vec[:, V_MU_R:V_MU_R + 2], -1.0, 1.0, ALU.mult, ALU.add)
            nc.vector.reciprocal(inv_scale[:, :], sc[:, 0:1])
            made = sem("made")
            tt(both_scales[:, :], sc[:, 0:1], sc[:, 1:2], ALU.mult).then_inc(made, 1)
            eight = w[:, W_CENTRED + 3 * P:W_CENTRED + 4 * P]
            dve.wait_ge(made, 1)
            ts(eight, eight, both_scales[:, 0:1], None, ALU.mult).then_inc(made, 1)
            dve.wait_ge(made, 2)
            four = w[:, W_CENTRED:W_CENTRED + 4 * P].rearrange("p (a n) -> p a n", a=4)
            nc.vector.tensor_reduce(row_sum[:, :], four, AXIS_X, ALU.add).then_inc(made, 1)
            dve.wait_ge(made, 3)
            ts(row_sum[:, :], row_sum[:, :], -1.0 / CHANNELS, None, ALU.mult).then_inc(made, 1)
            dve.wait_ge(made, 4)
            tt(four, four, row_sum[:, :].unsqueeze(2).broadcast_to([P, 4, P]), ALU.add).then_inc(made, 1)
            dve.wait_ge(made, 5)
            nc.vector.tensor_copy(w8[:, 0, :], eight).then_inc(made, 1)
            dve.wait_ge(made, 6)
            tt(w8_rest[:, :], eight, w8[:, 0, :], ALU.subtract).then_inc(made, 1)
            dve.wait_ge(made, 7)
            nc.vector.tensor_copy(w8[:, 1, :], w8_rest[:, :]).then_inc(made, 1)
            dve.wait_ge(made, 8)
            tt(w8_rest[:, :], w8_rest[:, :], w8[:, 1, :], ALU.subtract).then_inc(made, 1)
            dve.wait_ge(made, 9)
            chain(nc.vector.tensor_copy(w8[:, 2, :], w8_rest[:, :]))
            dve.wait_ge(prep, 4)

            with dve.Fori(0, SEQS // 2) as i:
                def total(k):
                    h = k % 2
                    dve.wait_ge(dt_ln, i * 4 + k + 1)
                    stt(out=decay[:, h, bass.ts(i * 2 + k // 2, CHUNK)], in0=bank[k], scalar=knee[:, h:h + 1],
                        in1=tmp[:, 4 + k, :], op0=ALU.max, op1=ALU.add).then_inc(dt_sum, 1)

                for k in range(4):
                    h = k % 2
                    dve.wait_ge(dt_ready, i * 4 + k + 1)
                    dve.wait_ge(dt_sum, i * 4 + k + 1)
                    ts(tmp[:, 4 + k, :], bank[k], vec[:, V_B_DT + h:V_B_DT + h + 1], SOFTPLUS_KNEE,
                       ALU.add, ALU.min).then_inc(dt_capped, 1)
                    if k >= 2:
                        total(k - 2)
                total(2)
                total(3)

            ops = 12
            with dve.Fori(0, SEQS // 2) as i:
                for k in range(2):
                    cols = bass.ts(i * 2 + k, CHUNK)
                    base = i * (2 * ops) + k * ops
                    halves = range(HALVES)
                    u = [tmp[:, 8 + h, :] for h in halves]
                    g = [tmp[:, 10 + h, :] for h in halves]
                    state = [tmp[:, 12 + h, :] for h in halves]
                    a = [decay[:, h, cols] for h in halves]
                    xc = [xconv[:, h, cols] for h in halves]
                    b_gate, c_gate = tmp[:, 2 * k, :], tmp[:, 2 * k + 1, :]
                    dve.wait_ge(gate_done, GATE0 + i * 4 + 2 * k + 2)
                    for h in halves:
                        tt(u[h], b_gate, xc[h], ALU.mult).then_inc(scan_step, 1)
                    for h in halves:
                        dve.wait_ge(alpha_done, i * 4 + 2 * k + h + 1)
                        dve.wait_ge(scan_step, base + h + 1)
                        stt(out=g[h], in0=a[h], scalar=-1.0, in1=u[h], op0=ALU.add, op1=ALU.mult).then_inc(scan_step, 1)
                    for h in halves:
                        dve.wait_ge(scan_step, base + 2 + h + 1)
                        ts(a[h], a[h], 0.01, 0.99, ALU.max, ALU.min).then_inc(scan_step, 1)
                    for h in halves:
                        dve.wait_ge(scan_step, base + 4 + h + 1)
                        nc.vector.tensor_tensor_scan(state[h], a[h], g[h], 0.0, ALU.mult, ALU.subtract).then_inc(scan_step, 1)
                    for h in halves:
                        dve.wait_ge(scan_step, base + 6 + h + 1)
                        tt(u[h], state[h], c_gate, ALU.mult).then_inc(scan_step, 1)
                    for h in halves:
                        dve.wait_ge(scan_step, base + 8 + h + 1)
                        stt(out=g[h], in0=xc[h], scalar=vec[:, V_D + h:V_D + h + 1], in1=u[h],
                            op0=ALU.mult, op1=ALU.add).then_inc(scan_step, 1)
                    for h in halves:
                        dve.wait_ge(scan_step, base + 10 + h + 1)
                        tt(xc[h], g[h], silu_z[:, h, cols], ALU.mult).then_inc(y_done, 1)

            dve.wait_ge(y_done, Y0 + 2 * SEQS)
            quant_ops = 4
            with dve.Fori(0, CHUNKS // 4) as i:
                def normed(out, source, n, k):
                    dve.wait_ge(rstd_done, i * 12 + n * 4 + k + 1)
                    return tt(out, source, rstd[:, k, :], ALU.mult)

                def rounding(k):
                    xk, mk = xs[:, k, :], step8[:, k, :]
                    at = i * 16 + k * quant_ops
                    dve.wait_ge(xs_done, i * 4 + k + 1)
                    ts(xk, xk, FP8_MAX, -FP8_MAX, ALU.min, ALU.max).then_inc(quant_step, 1)
                    dve.wait_ge(quant_step, at + 1)
                    ts(mk.bitcast(I32), xk.bitcast(I32), 0x7F800000, None, ALU.bitwise_and).then_inc(quant_step, 1)
                    dve.wait_ge(quant_step, at + 2)
                    ts(mk, mk, 2.0 ** -6, 1.5 * 2.0 ** 20, ALU.max, ALU.mult).then_inc(quant_step, 1)
                    dve.wait_ge(quant_step, at + 3)
                    tt(xk, xk, mk, ALU.add).then_inc(quant_step, 1)
                    dve.wait_ge(quant_step, at + 4)
                    tt(quant[:, k, :], xk, mk, ALU.subtract).then_inc(quant_done, 1)

                for k in range(4):
                    normed(x1[:, k, :], bank[k], 0, k).then_inc(x1_done, 1)
                    if k:
                        rounding(k - 1)
                rounding(3)

                def y2(k):
                    dve.wait_ge(ffn_ready, i * 4 + k + 1)
                    stt(out=x2[:, k, :], in0=bank[6 + k % 2], scalar=centred_bias[:, 0:1], in1=x1[:, k, :],
                        op0=ALU.add, op1=ALU.add).then_inc(y2_done, 1)

                for k in range(4):
                    y2(k)
                    if k >= 2:
                        normed(x2[:, k - 2, :], x2[:, k - 2, :], 1, k - 2).then_inc(x2_done, 1)
                for k in range(2, 4):
                    normed(x2[:, k, :], x2[:, k, :], 1, k).then_inc(x2_done, 1)
                for k in range(4):
                    dve.wait_ge(v_ready, i * 4 + k + 1)
                    nc.vector.tensor_copy(v[:, k, :], bank[(6 + 3 * k) % 4]).then_inc(v_done, 1)

                def logits(k):
                    dve.wait_ge(score_ready, i * 4 + k + 1)
                    tt(grouped(prob[:, k, :]), grouped(bank[6 + k % 2]), mask_all_groups, ALU.min).then_inc(logit_done, 1)
                    dve.wait_ge(logit_done, LOGIT0 + i * 4 + k + 1)
                    nc.vector.tensor_reduce(neg_max[:, k, :], grouped(prob[:, k, :]), AXIS_X, ALU.max).then_inc(max_step, 1)
                    dve.wait_ge(max_step, i * 4 + k + 1)
                    ts(neg_max[:, k, :], neg_max[:, k, :], -1.0, None, ALU.mult).then_inc(neg_max_done, 1)

                def normalise(k):
                    dve.wait_ge(exp_done, i * 4 + k + 1)
                    nc.vector.reciprocal(inv_sum[:, k, :], exp_sum[:, k, :]).then_inc(inv_done, 1)
                    dve.wait_ge(inv_done, i * 4 + k + 1)
                    pk = grouped(prob[:, k, :])
                    tt(pk, pk, inv_sum[:, k, :].unsqueeze(2).broadcast_to([P, GROUPS, P]), ALU.mult).then_inc(prob_done, 1)

                for k in range(4):
                    logits(k)
                    if k:
                        normalise(k - 1)
                normalise(3)

                for k in range(4):
                    dve.wait_ge(att_ready, i * 4 + k + 1)
                    stt(out=y3[:, k, :], in0=bank[2 + k % 2], scalar=centred_bias[:, 1:2], in1=x2[:, k, :],
                        op0=ALU.add, op1=ALU.add).then_inc(y3_done, 1)
                    if k >= 2:
                        dve.wait_ge(rstd_done, i * 12 + 8 + k - 1)
                        tt(x3_chunks[:, i * 4 + k - 2], by_position(y3[:, k - 2, :]), by_position(rstd[:, k - 2, :]),
                           ALU.mult).then_inc(x3_done, 1)
                for k in range(2, 4):
                    dve.wait_ge(rstd_done, i * 12 + 8 + k + 1)
                    tt(x3_chunks[:, i * 4 + k], by_position(y3[:, k, :]), by_position(rstd[:, k, :]),
                       ALU.mult).then_inc(x3_done, 1)

            dve.wait_ge(x3_done, X3_0 + CHUNKS)
            with dve.Fori(0, SEQS // 2) as i:
                for k in range(2):
                    b = i * 2 + k
                    now, before = x3[:, b, 1:LENGTH + 1], x3[:, b, 0:LENGTH]
                    tt(tmp[:, k, :], before, now, ALU.subtract).then_inc(shift_done, 1)
                for k in range(2):
                    b = i * 2 + k
                    now = x3[:, b, 1:LENGTH + 1]
                    dve.wait_ge(shift_done, b + 1)
                    dve.wait_ge(r_done, b + 1)
                    stt(out=tmp[:, 2 + k, :], in0=tmp[:, k, :], scalar=one_minus_mu[:, 0:1], in1=now,
                        op0=ALU.mult, op1=ALU.add).then_inc(xr_done, 1)
                    dve.wait_ge(relu_done, b + 1)
                    stt(out=tmp[:, 4 + k, :], in0=tmp[:, k, :], scalar=one_minus_mu[:, 1:2], in1=now,
                        op0=ALU.mult, op1=ALU.add).then_inc(xk_done, 1)
                for k in range(2):
                    b = i * 2 + k
                    dve.wait_ge(r_done, SMALL0 + b + 1)
                    dve.wait_ge(fv_ready, b + 1)
                    dve.wait_ge(cen_done, b + 1)
                    tt(tmp[:, 12 + k, :], bank[4 + k], tmp[:, 6 + k, :], ALU.mult).then_inc(rv_done, 1)
                for k in range(2):
                    b = i * 2 + k
                    dve.wait_ge(rv_done, SMALL0 + b + 1)
                    tt(tmp[:, 12 + k, :], tmp[:, 12 + k, :], x3[:, b, 1:LENGTH + 1], ALU.add).then_inc(sum_done, 1)
            with dve.Fori(0, SEQS // 2) as i:
                for k in range(2):
                    b = i * 2 + k
                    dve.wait_ge(last_rstd, b + 1)
                    tt(decay[:, 0, bass.ts(b, CHUNK)], xT[:, bass.ts(b, CHUNK)], tmp[:, 8 + k, :], ALU.mult).then_inc(last_out, 1)


def kernel(**inputs):
    import numpy as np
    import concourse.bacc as bacc
    from concourse.bass_utils import run_bass_kernel_spmd

    a = {k: np.asarray(v) for k, v in inputs.items()}

    def halves(m):
        return m.reshape(HALVES, P, -1).transpose(1, 0, 2).reshape(P, -1)

    weights = np.concatenate([
        halves(a["L0_attn_W_x"][2 * STATE:]), halves(a["L0_attn_W_dt"].T), halves(a["L0_attn_W_out"].T),
        a["L1_attn_Wv"].T, a["L0_ffn_weight_fp8"].T, a["L1_attn_Wq"].T, a["L1_attn_Wk"].T,
        a["L1_ffn_W_r"].T, a["L1_ffn_W_k"].T, a["L1_ffn_W_v"].T], axis=1)
    columns = [halves(a["L0_attn_conv_w"].reshape(INNER, TAPS))]
    columns += [halves(a[n].reshape(INNER, 1)) for n in ("L0_attn_conv_b", "L0_attn_b_dt", "L0_attn_D")]
    columns += [a[n].reshape(P, 1) for n in ("L0_ffn_bias", "L1_attn_bv", "L1_attn_bq", "L1_attn_bk",
                                             "L1_ffn_mu_r", "L1_ffn_mu_k")]
    position = np.arange(P) % GROUP
    same = position[:, None] == position[None, :]
    eye = np.eye(P, dtype=np.float32)
    constants = np.concatenate([eye, eye - np.float32(1.0 / CHANNELS),
                                np.where(same, 0.0, MASKED).astype(np.float32)], axis=1)
    arrays = {
        "x_t": a["L0_attn_x"].reshape(TOKENS, CHANNELS).T,
        "w_in_t": a["L0_attn_W_in"].T,
        "vectors": np.concatenate(columns, axis=1),
        "weights": weights,
        "gate_rows": a["L0_attn_W_x"][:2 * STATE].reshape(2, STATE, INNER).transpose(1, 0, 2),
        "scales": np.concatenate([a["L0_ffn_input_scale"], a["L0_ffn_weight_scale"]]),
        "constants": constants,
    }
    arrays = {k: np.ascontiguousarray(v) for k, v in arrays.items()}
    nc = bacc.Bacc("TRN2", target_bir_lowering=False, num_devices=1)
    args = [nc.dram_tensor(k, v.shape, mybir.dt.from_np(v.dtype), kind="ExternalInput").ap() for k, v in arrays.items()]
    args.append(nc.dram_tensor("out_t", (CHANNELS, TOKENS), F32, kind="ExternalOutput").ap())
    build(nc, *args)
    r = run_bass_kernel_spmd(nc, [arrays], core_ids=[0])
    out = r.results[0]["out_t"]
    return np.ascontiguousarray(out.T).reshape(SEQS, LENGTH, CHANNELS)
```

```python
from contextlib import ExitStack

import concourse.bass as bass
from concourse import mybir

ALU = mybir.AluOpType
ACT = mybir.ActivationFunctionType
AXIS_X = mybir.AxisListType.X
F32 = mybir.dt.float32
BF16 = mybir.dt.bfloat16
I32 = mybir.dt.int32

P = 128
SEQS, LENGTH, CHANNELS = 8, 512, 128
TOKENS = SEQS * LENGTH
HALVES = 2
INNER = HALVES * P
TAPS = 4
STATE = 16
CHUNK = 512
SPAN = CHUNK // SEQS
GROUP = P // SEQS
GROUPS = CHUNK // P
CHUNKS = TOKENS // CHUNK
EPS = 1e-5
FP8_MAX = 448.0
SOFTPLUS_KNEE = 20.0
MASKED = 1e30

W_COMB_X = 0
W_COMB_DT = W_COMB_X + HALVES * INNER
W_CENTRED = W_COMB_DT + HALVES * INNER
W_Q = W_CENTRED + 4 * P
W_K = W_Q + P
W_FR = W_K + P
W_FK = W_FR + P
W_FV = W_FK + P
W_COLS = W_FV + P
V_CONV_W = 0
V_CONV_B = V_CONV_W + HALVES * TAPS
V_B_DT = V_CONV_B + HALVES
V_D = V_B_DT + HALVES
V_BIAS8 = V_D + HALVES
V_BV = V_BIAS8 + 1
V_BQ = V_BV + 1
V_BK = V_BQ + 1
V_MU_R = V_BK + 1
V_MU_K = V_MU_R + 1
V_COLS = V_MU_K + 1
C_IDENT = 0
C_CENTRE = P
C_MASK = 2 * P
C_COLS = 3 * P


def build(nc, x_t, w_in_t, vectors, weights, gate_rows, scales, constants, out_t):
    with ExitStack() as ctx:
        def sb(name, shape, dt=F32):
            return ctx.enter_context(nc.sbuf_tensor(name, shape, dt))

        def sem(name):
            return ctx.enter_context(nc.semaphore(name))

        xT = sb("xT", [P, TOKENS])
        xconv = sb("xconv", [P, CHUNKS, HALVES, CHUNK])
        silu_z = sb("silu_z", [P, CHUNKS, HALVES, CHUNK])
        decay = sb("decay", [P, CHUNKS, HALVES, CHUNK])
        state = sb("state", [P, CHUNKS, HALVES, CHUNK])
        c_gate = sb("c_gate", [P, CHUNKS, CHUNK])

        w_in = sb("w_in", [P, 2 * INNER])
        vec = sb("vec", [P, V_COLS])
        w = sb("w", [P, W_COLS])
        gate_w = sb("gate_w", [STATE, 2, INNER])
        sc = sb("sc", [P, 2])
        const = sb("const", [P, C_COLS])
        comb = sb("comb", [P, HALVES, INNER])
        gates = sb("gates", [P, 2, HALVES, P])
        w8 = sb("w8", [P, 3, P], BF16)
        w8_rest = sb("w8_rest", [P, P])
        sixteenth = sb("sixteenth", [STATE, P])
        mean_w = sb("mean_w", [P, P])
        half_w = sb("half_w", [P, P])
        row_sum = sb("row_sum", [P, 4])
        both_scales = sb("both_scales", [P, 1])
        inv_scale = sb("inv_scale", [P, 1])
        knee = sb("knee", [P, HALVES])
        alpha_bias = sb("alpha_bias", [P, HALVES])
        one_minus_mu = sb("one_minus_mu", [P, 2])
        minus_bq = sb("minus_bq", [P, 1])
        centred_bias = sb("centred_bias", [P, 2])
        eps = sb("eps", [P, 1])
        credit = sb("credit", [P, 16])
        carried = sb("carried", [P, HALVES, SEQS])
        entering = sb("entering", [P, HALVES, SEQS])
        least = sb("least", [P, CHUNKS, GROUPS])
        exp_sum = sb("exp_sum", [P, CHUNKS, GROUPS])
        inv_sum = sb("inv_sum", [P, CHUNKS, GROUPS])

        ident = const[:, C_IDENT:C_IDENT + P]
        centre = const[:, C_CENTRE:C_CENTRE + P]
        mask = const[:, C_MASK:C_MASK + P]
        mask_all_groups = mask.unsqueeze(1).broadcast_to([P, GROUPS, P])

        def by_sequence(array):
            return array[:, :, :, :].rearrange("p c h (b l) -> p b h c l", b=SEQS)

        xconv_s, silu_z_s, decay_s, state_s = (by_sequence(t) for t in (xconv, silu_z, decay, state))

        def along(ap):
            return ap.rearrange("p (c l) -> p c l", c=CHUNKS)

        y_groups = state[:, :, :, :].rearrange("p c h (b g l) -> p c h g b l", b=SEQS, g=GROUPS)
        x_groups = xT[:, :].rearrange("p (b c g l) -> p c g b l", b=SEQS, c=CHUNKS, g=GROUPS)
        x_chunks = xT[:, :].rearrange("p (b c l) -> p c b l", b=SEQS, c=CHUNKS)

        def grouped(ap):
            return ap.rearrange("p (g n) -> p g n", g=GROUPS)

        def by_position(ap):
            return ap.rearrange("p (g b l) -> p g b l", g=GROUPS, b=SEQS)

        def in_chunk(ap):
            return ap.rearrange("p (b l) -> p b l", b=SEQS)

        def tiles(array, half):
            return [array[:, c, half, :] for c in range(CHUNKS)]

        x1 = prob = xk = tiles(xconv, 0)
        xs = v = k_act = tiles(xconv, 1)
        step8 = k_ = k_relu = tiles(decay, 0)
        quant = [t.bitcast(BF16)[:, 0:CHUNK] for t in tiles(decay, 1)]
        k_sq = xr = tiles(decay, 1)
        sq = x_diff = tiles(silu_z, 0)
        rstd = tiles(silu_z, 1)
        x2 = result = [c_gate[:, c, :] for c in range(CHUNKS)]
        q = prob_t = r = tiles(state, 0)
        q_sq = y3 = y4 = tiles(state, 1)

        psum = ctx.enter_context(nc.psum_tensor("psum", [P, 8, CHUNK], F32))
        bank = [psum[:, n, :] for n in range(8)]
        OUT_BANK, VAR_BANK, CEN_BANK, V_BANK, ATT_BANK, Q_BANK, TURN_BANK, FFN_BANK, K_BANK, FK_BANK, FV_BANK, FR_BANK, SCORE_BANK = 0, 1, 2, 3, 3, 4, 4, 5, 5, 6, 6, 7, 7

        x_first, x_rest, small_in, weights_in = sem("x_first"), sem("x_rest"), sem("small_in"), sem("weights_in")
        filled = sem("filled")
        prep_mm, prep, made, clipped = (sem(n) for n in ("prep_mm", "prep", "made", "clipped"))
        xp_ready, z_ready, tap_done, conv_step, conv_done, xconv_done, z_done = (
            sem(n) for n in ("xp_ready", "z_ready", "tap_done", "conv_step", "conv_done", "xconv_done", "z_done"))
        dt_ready, dt_capped, dt_exp, dt_ln, dt_sum = (sem(n) for n in ("dt_ready", "dt_capped", "dt_exp", "dt_ln", "dt_sum"))
        gate_ready, gate_done, alpha_done, gated_step, gated_done = (
            sem(n) for n in ("gate_ready", "gate_done", "alpha_done", "gated_step", "gated_done"))
        entering_done, edge_done, scan_done, carry_done, cgated, skip_done, y_done = (
            sem(n) for n in ("entering_done", "edge_done", "scan_done", "carry_done", "cgated", "skip_done", "y_done"))
        out_ready, x1_done, xs_done, quant_step, quant_done = (
            sem(n) for n in ("out_ready", "x1_done", "xs_done", "quant_step", "quant_done"))
        sq_done, var_ready, var_read, rstd_done = (
            [sem(f"{n}{m + 1}") for m in range(4)] for n in ("sq_done", "var_ready", "var_read", "rstd_done"))
        ffn_ready, y2_done, x2_done = sem("ffn_ready"), sem("y2_done"), sem("x2_done")
        q_ready, k_ready, v_ready, q_done, k_done, v_done = (
            sem(n) for n in ("q_ready", "k_ready", "v_ready", "q_done", "k_done", "v_done"))
        score_ready, logit_done, least_done, exp_done, inv_done, prob_done = (
            sem(n) for n in ("score_ready", "logit_done", "least_done", "exp_done", "inv_done", "prob_done"))
        turned_ready, turned_done, att_ready, y3_done, x3_done = (
            sem(n) for n in ("turned_ready", "turned_done", "att_ready", "y3_done", "x3_done"))
        diff_done, xk_done, xr_done, fk_ready, relu_done, kact_done = (
            sem(n) for n in ("diff_done", "xk_done", "xr_done", "fk_ready", "relu_done", "kact_done"))
        fr_ready, r_exp, r_ln, r_done, fv_ready, rv_done, y4_done, cen_ready, out_done, stored = (
            sem(n) for n in ("fr_ready", "r_exp", "r_ln", "r_done", "fv_ready", "rv_done", "y4_done", "cen_ready",
                             "out_done", "stored"))

        RING = 4

        block = ctx.enter_context(nc.Block())

        def sequences(eng, unit, last):
            unit(0, 0, False)
            with eng.Fori(0, SEQS // 2 - 1) as i:
                unit(i * 2 + 1, 1, True)
                unit(i * 2 + 2, 0, True)
            unit(SEQS - 1, 1, True)
            last(SEQS - 1, 1)

        STEPS = CHUNKS + 10

        def pipeline(*work):
            for t in range(STEPS):
                for lag, stage in work:
                    if 0 <= t - lag < CHUNKS:
                        stage(t - lag)

        @block.sync
        def _(sp):
            first_x = 2 * CHUNK
            sp.dma_start(w_in[:, :], w_in_t).then_inc(small_in, 16)
            sp.dma_start(xT[:, 0:first_x], x_t[:, 0:first_x]).then_inc(x_first, 16)
            sp.dma_start(xT[:, first_x:], x_t[:, first_x:]).then_inc(x_rest, 16)
            sp.dma_start(w[:, :], weights).then_inc(weights_in, 16)
            sp.dma_start(const[:, :], constants).then_inc(weights_in, 16)
            sp.dma_start(gate_w[:, :, :], gate_rows).then_inc(weights_in, 16)
            sp.dma_start(sc[:, :], scales.rearrange("(a n) -> a n", a=1).broadcast_to([P, 2])).then_inc(weights_in, 16)
            with sp.Fori(0, CHUNKS // 2) as i:
                for k in range(2):
                    c = i * 2 + k
                    sp.wait_ge(out_done, c + 1)
                    sp.dma_start(out_t[:, bass.ts(c, CHUNK)], c_gate[:, c, :]).then_inc(stored, 16)
            sp.wait_ge(stored, 16 * CHUNKS)

        @block.tensor
        def _(pe):
            def mm(out, lhs_t, rhs, first=True, last=True, open_group=False):
                return nc.tensor.matmul(out, lhs_t, rhs, start=first, stop=last, skip_group_check=open_group)

            pe.wait_ge(small_in, 32)
            pe.wait_ge(x_first, 16)
            pe.wait_ge(filled, 1)
            with pe.Fori(0, SEQS // 2) as i:
                for k in range(2 * HALVES):
                    j = i * 4 + k
                    b, h = i * 2 + k // 2, k % 2
                    if k == 0:
                        pe.wait_ge(x_first, 16)
                    if k == 2:
                        pe.wait_ge(x_rest, 16)
                    pe.wait_ge(conv_done, j + 1)
                    mm(bank[k], w_in[:, h * P:(h + 1) * P], xT[:, bass.ts(b, CHUNK)]).then_inc(xp_ready, 1)
                    pe.wait_ge(z_done, j + 1)
                    mm(bank[4 + k], w_in[:, INNER + h * P:INNER + (h + 1) * P],
                       xT[:, bass.ts(b, CHUNK)]).then_inc(z_ready, 1)

            pe.wait_ge(weights_in, 64)
            pe.wait_ge(z_done, RING + 2 * SEQS)
            for ih in range(HALVES):
                for mh in range(HALVES):
                    last = mm(bank[4 + ih][:, 0:INNER],
                              w[:, W_COMB_X + mh * INNER + ih * P:W_COMB_X + mh * INNER + (ih + 1) * P],
                              w[:, W_COMB_DT + mh * INNER:W_COMB_DT + (mh + 1) * INNER], mh == 0, mh == 1)
            last.then_inc(prep_mm, 1)
            for gate in range(2):
                for ih in range(HALVES):
                    last = mm(bank[6][:, (2 * gate + ih) * P:(2 * gate + ih + 1) * P],
                              gate_w[:, gate, ih * P:(ih + 1) * P], sixteenth[:, :])
            last.then_inc(prep_mm, 1)
            mm(bank[7][:, 0:2], centre, vec[:, V_BIAS8:V_BIAS8 + 2]).then_inc(prep_mm, 1)

            pe.wait_ge(prep, 1)
            pe.wait_ge(conv_done, RING + 2 * SEQS)
            with pe.Fori(0, SEQS // 2) as i:
                for k in range(2 * HALVES):
                    b, h = i * 2 + k // 2, k % 2
                    pe.wait_ge(xconv_done, RING + i * 4 + 2 * (k // 2) + 2)
                    pe.wait_ge(dt_sum, i * 4 + k + 1)
                    for ih in range(HALVES):
                        last = mm(along(bank[k]), comb[:, ih, h * P:(h + 1) * P], xconv_s[:, b, ih], ih == 0, ih == 1)
                    last.then_inc(dt_ready, 1)

            pe.wait_ge(prep, 3)
            with pe.Fori(0, CHUNKS // 2) as i:
                for k in range(2):
                    c = i * 2 + k
                    for gate in range(2):
                        pe.wait_ge(gate_done, i * 4 + 2 * k + gate + 1)
                        for ih in range(HALVES):
                            last = mm(bank[4 + 2 * k + gate], gates[:, gate, ih, :], xconv[:, c, ih, :], ih == 0, ih == 1)
                        last.then_inc(gate_ready, 1)

            free = [(dt_sum, RING + 2 * SEQS)] * 4 + [(gate_done, RING + 2 * CHUNKS)] * 4

            def out_proj(c):
                pe.wait_ge(y_done, c + 1)
                pe.wait_ge(*free[OUT_BANK])
                for h in range(HALVES):
                    mm(by_position(bank[OUT_BANK]), w[:, W_CENTRED + h * P:W_CENTRED + (h + 1) * P], y_groups[:, c, h], h == 0, False)
                mm(by_position(bank[OUT_BANK]), centre, x_groups[:, c], False, True).then_inc(out_ready, 1)
                free[OUT_BANK] = (x1_done, c + 1)

            def variance(n):
                def of(c):
                    pe.wait_ge(sq_done[n], c + 1)
                    pe.wait_ge(*free[VAR_BANK])
                    mm(bank[VAR_BANK], mean_w[:, :], sq[c]).then_inc(var_ready[n], 1)
                    free[VAR_BANK] = (var_read[n], c + 1)
                return of

            var1, var2, var3, var4 = (variance(n) for n in range(4))

            def ffn(c):
                pe.wait_ge(quant_done, c + 1)
                pe.wait_ge(*free[FFN_BANK])
                for part in range(3):
                    last = mm(bank[FFN_BANK], w8[:, part, :], quant[c], part == 0, part == 2)
                last.then_inc(ffn_ready, 1)
                free[FFN_BANK] = (y2_done, c + 1)

            def queries(c):
                pe.wait_ge(x2_done, c + 1)
                pe.wait_ge(*free[Q_BANK])
                mm(bank[Q_BANK], w[:, W_Q:W_Q + P], x2[c]).then_inc(q_ready, 1)
                free[Q_BANK] = (q_done, c + 1)

            def keys(c):
                pe.wait_ge(x2_done, c + 1)
                pe.wait_ge(*free[K_BANK])
                mm(bank[K_BANK], w[:, W_K:W_K + P], x2[c]).then_inc(k_ready, 1)
                free[K_BANK] = (k_done, c + 1)

            def values(c):
                pe.wait_ge(x2_done, c + 1)
                pe.wait_ge(*free[V_BANK])
                for g in range(GROUPS):
                    cols = slice(g * P, (g + 1) * P)
                    last = mm(bank[V_BANK][:, cols], x2[c][:, cols], w[:, W_CENTRED + 2 * P:W_CENTRED + 3 * P])
                last.then_inc(v_ready, 1)
                free[V_BANK] = (v_done, c + 1)

            def scores(c):
                s = bank[SCORE_BANK]
                pe.wait_ge(q_done, c + 1)
                pe.wait_ge(k_done, c + 1)
                pe.wait_ge(*free[SCORE_BANK])
                mm(s, half_w[:, :], k_sq[c], True, False, True)
                for g in range(GROUPS):
                    cols = slice(g * P, (g + 1) * P)
                    mm(s[:, cols], q_sq[c][:, cols], half_w[:, :], False, False, True)
                    last = mm(s[:, cols], q[c][:, cols], k_[c][:, cols], False, True, True)
                last.then_inc(score_ready, 1)
                free[SCORE_BANK] = (logit_done, c + 1)

            def turn(c):
                pe.wait_ge(prob_done, c + 1)
                pe.wait_ge(*free[TURN_BANK])
                for g in range(GROUPS):
                    cols = slice(g * P, (g + 1) * P)
                    last = nc.tensor.transpose(bank[TURN_BANK][:, cols], prob[c][:, cols], ident)
                last.then_inc(turned_ready, 1)
                free[TURN_BANK] = (turned_done, c + 1)

            def attend(c):
                pe.wait_ge(turned_done, c + 1)
                pe.wait_ge(v_done, c + 1)
                pe.wait_ge(*free[ATT_BANK])
                for g in range(GROUPS):
                    cols = slice(g * P, (g + 1) * P)
                    last = mm(bank[ATT_BANK][:, cols], v[c][:, cols], prob_t[c][:, cols])
                last.then_inc(att_ready, 1)
                free[ATT_BANK] = (y3_done, c + 1)

            def mix_keys(c):
                pe.wait_ge(xk_done, c + 1)
                pe.wait_ge(*free[FK_BANK])
                mm(bank[FK_BANK], w[:, W_FK:W_FK + P], xk[c]).then_inc(fk_ready, 1)
                free[FK_BANK] = (relu_done, c + 1)

            def mix_gate(c):
                pe.wait_ge(xr_done, c + 1)
                pe.wait_ge(*free[FR_BANK])
                mm(bank[FR_BANK], w[:, W_FR:W_FR + P], xr[c]).then_inc(fr_ready, 1)
                free[FR_BANK] = (r_exp, c + 1)

            def mix_values(c):
                pe.wait_ge(kact_done, c + 1)
                pe.wait_ge(*free[FV_BANK])
                mm(bank[FV_BANK], w[:, W_FV:W_FV + P], k_act[c]).then_inc(fv_ready, 1)
                free[FV_BANK] = (rv_done, c + 1)

            def centre4(c):
                pe.wait_ge(y4_done, c + 1)
                pe.wait_ge(*free[CEN_BANK])
                mm(bank[CEN_BANK], centre, y4[c]).then_inc(cen_ready, 1)
                free[CEN_BANK] = (out_done, c + 1)

            pe.wait_ge(prep, 4)
            pipeline((7, ffn), (9, var3), (8, scores), (7, var2), (10, centre4), (5, out_proj), (10, var4),
                     (9, mix_keys), (7, keys), (8, turn), (5, var1), (9, mix_gate), (8, attend), (9, mix_values),
                     (7, queries), (7, values))

        @block.scalar
        def _(act):
            act.dma_start(vec[:, :], vectors).then_inc(small_in, 16)
            acc = [state[:, n // 2, n % 2, :] for n in range(8)]

            nc.scalar.preload_act_table(ACT.Silu)
            act.wait_ge(small_in, 32)

            def conv_silu(b, slot):
                for h in range(HALVES):
                    act.wait_ge(conv_done, RING + b * 2 + h + 1)
                    nc.scalar.activation(xconv_s[:, b, h], along(acc[2 * slot + h]), ACT.Silu).then_inc(xconv_done, 1)

            def unit_a(b, slot, previous):
                for h in range(HALVES):
                    j, k = b * 2 + h, 2 * slot + h
                    act.wait_ge(xp_ready, j + 1)
                    act.wait_ge(xconv_done, j + 1)
                    nc.scalar.activation(acc[k], bank[k], ACT.Identity,
                                         bias=vec[:, V_CONV_B + h:V_CONV_B + h + 1],
                                         scale=vec[:, V_CONV_W + h * TAPS + 3:V_CONV_W + h * TAPS + 4]).then_inc(tap_done, 1)
                    act.wait_ge(z_ready, j + 1)
                    nc.scalar.activation(silu_z_s[:, b, h], along(bank[4 + k]), ACT.Silu).then_inc(z_done, 1)
                if previous:
                    conv_silu(b - 1, 1 - slot)

            sequences(act, unit_a, conv_silu)

            nc.scalar.preload_act_table_set("natural_log_exp_and_others")
            with act.Fori(0, SEQS // 2) as i:
                for slot in range(2):
                    for h in range(HALVES):
                        k = 2 * slot + h
                        act.wait_ge(dt_capped, i * 4 + k + 1)
                        nc.scalar.activation(acc[4 + k], acc[4 + k], ACT.Exp).then_inc(dt_exp, 1)
                    for h in range(HALVES):
                        k = 2 * slot + h
                        act.wait_ge(dt_exp, i * 4 + k + 1)
                        nc.scalar.activation(acc[4 + k], acc[4 + k], ACT.Ln, bias=1.0).then_inc(dt_ln, 1)

            nc.scalar.preload_act_table(ACT.Sigmoid)
            act.wait_ge(dt_sum, RING + 2 * SEQS)
            with act.Fori(0, CHUNKS // 2) as i:
                for k in range(2):
                    c = i * 2 + k
                    for h in range(HALVES):
                        a = decay[:, c, h, :]
                        nc.scalar.activation(a, a, ACT.Sigmoid, bias=alpha_bias[:, h:h + 1], scale=0.1).then_inc(alpha_done, 1)
                    act.wait_ge(gate_ready, i * 4 + 2 * k + 1)
                    nc.scalar.activation(state[:, c, 0, :], bank[4 + 2 * k], ACT.Sigmoid).then_inc(gate_done, 1)
                    act.wait_ge(gate_ready, i * 4 + 2 * k + 2)
                    nc.scalar.activation(c_gate[:, c, :], bank[5 + 2 * k], ACT.Sigmoid).then_inc(gate_done, 1)

            nc.scalar.preload_act_table_set("natural_log_exp_and_others")

            def square(n):
                def of(c):
                    source, ready = ((bank[OUT_BANK], out_ready), (x2[c], y2_done), (y3[c], y3_done),
                                     (bank[CEN_BANK], cen_ready))[n]
                    act.wait_ge(ready, c + 1)
                    nc.scalar.activation(sq[c], source, ACT.Square).then_inc(sq_done[n], 1)
                return of

            def inv_std(n):
                def of(c):
                    act.wait_ge(var_ready[n], c + 1)
                    nc.scalar.activation(rstd[c], bank[VAR_BANK], ACT.Ln, bias=eps[:, 0:1]).then_inc(var_read[n], 1)
                    act.wait_ge(var_read[n], c + 1)
                    nc.scalar.activation(rstd[c], rstd[c], ACT.Exp, scale=-0.5).then_inc(rstd_done[n], 1)
                return of

            square1, square2, square3, square4 = (square(n) for n in range(4))
            inv_std1, inv_std2, inv_std3, inv_std4 = (inv_std(n) for n in range(4))

            def rescale(c):
                act.wait_ge(x1_done, c + 1)
                nc.scalar.activation(xs[c], x1[c], ACT.Identity, scale=inv_scale[:, 0:1]).then_inc(xs_done, 1)

            def keep_queries(c):
                act.wait_ge(q_ready, c + 1)
                nc.scalar.activation(q[c], bank[Q_BANK], ACT.Identity, bias=minus_bq[:, 0:1], scale=-1.0)
                nc.scalar.activation(q_sq[c], bank[Q_BANK], ACT.Square, bias=vec[:, V_BQ:V_BQ + 1]).then_inc(q_done, 1)

            def keep_keys(c):
                act.wait_ge(k_ready, c + 1)
                nc.scalar.activation(k_[c], bank[K_BANK], ACT.Identity, bias=vec[:, V_BK:V_BK + 1])
                nc.scalar.activation(k_sq[c], bank[K_BANK], ACT.Square, bias=vec[:, V_BK:V_BK + 1]).then_inc(k_done, 1)

            def keep_values(c):
                act.wait_ge(v_ready, c + 1)
                nc.scalar.activation(v[c], bank[V_BANK], ACT.Copy).then_inc(v_done, 1)

            def softmax_exp(c):
                act.wait_ge(least_done, c + 1)
                for g in range(GROUPS):
                    cols = slice(g * P, (g + 1) * P)
                    e = nc.scalar.activation(prob[c][:, cols], prob[c][:, cols], ACT.Exp, bias=least[:, c, g:g + 1],
                                             scale=-1.0, accum_out=exp_sum[:, c, g:g + 1])
                e.then_inc(exp_done, 1)

            def keep_turned(c):
                act.wait_ge(turned_ready, c + 1)
                nc.scalar.activation(prob_t[c], bank[TURN_BANK], ACT.Copy).then_inc(turned_done, 1)

            def relu_squared(c):
                act.wait_ge(fk_ready, c + 1)
                nc.scalar.activation(k_relu[c], bank[FK_BANK], ACT.Relu).then_inc(relu_done, 1)
                act.wait_ge(relu_done, c + 1)
                nc.scalar.activation(k_act[c], k_relu[c], ACT.Square).then_inc(kact_done, 1)

            def gate_sigmoid(c):
                act.wait_ge(fr_ready, c + 1)
                nc.scalar.activation(r[c], bank[FR_BANK], ACT.Exp, scale=-1.0).then_inc(r_exp, 1)
                act.wait_ge(r_exp, c + 1)
                nc.scalar.activation(r[c], r[c], ACT.Ln, bias=1.0).then_inc(r_ln, 1)
                act.wait_ge(r_ln, c + 1)
                nc.scalar.activation(r[c], r[c], ACT.Exp, scale=-1.0).then_inc(r_done, 1)

            pipeline((9, square3), (8, keep_queries), (9, inv_std3), (7, square2), (6, rescale), (8, keep_values),
                     (7, inv_std2), (10, square4), (8, softmax_exp), (5, square1), (10, inv_std4), (9, relu_squared),
                     (8, keep_turned), (7, keep_keys), (5, inv_std1), (9, gate_sigmoid))

        @block.vector
        def _(dve):
            tt, ts, stt = nc.vector.tensor_tensor, nc.vector.tensor_scalar, nc.vector.scalar_tensor_tensor
            acc = [state[:, n // 2, n % 2, :] for n in range(8)]

            nc.vector.memset(sixteenth[:, :], 1.0 / STATE)
            nc.vector.memset(mean_w[:, :], 1.0 / CHANNELS)
            nc.vector.memset(half_w[:, :], 0.5)
            nc.vector.memset(eps[:, :], EPS).then_inc(filled, 1)
            for at, ring in enumerate((conv_done, z_done, xconv_done, dt_sum, gate_done)):
                nc.vector.memset(credit[:, at:at + 1], 0.0).then_inc(ring, RING)

            dve.wait_ge(small_in, 32)
            with dve.Fori(0, SEQS // 2) as i:
                for slot in range(2):
                    for tap in (2, 1, 0):
                        shift = TAPS - 1 - tap
                        for h in range(HALVES):
                            k = 2 * slot + h
                            if tap == 2:
                                dve.wait_ge(tap_done, i * 4 + k + 1)
                            else:
                                dve.wait_ge(conv_step, i * 8 + 4 * slot + 2 * (1 - tap) + h + 1)
                            part = acc[k][:, shift:]
                            col = V_CONV_W + h * TAPS + tap
                            done = stt(out=part, in0=bank[k][:, 0:CHUNK - shift], scalar=vec[:, col:col + 1], in1=part,
                                       op0=ALU.mult, op1=ALU.add)
                            done.then_inc(conv_done if tap == 0 else conv_step, 1)

            dve.wait_ge(weights_in, 64)
            dve.wait_ge(prep_mm, 1)
            nc.vector.tensor_copy(comb[:, :, :], psum[:, 4:6, 0:INNER]).then_inc(prep, 1)
            ts(knee[:, :], vec[:, V_B_DT:V_B_DT + 2], -1.0, SOFTPLUS_KNEE, ALU.mult, ALU.add).then_inc(made, 1)
            ts(alpha_bias[:, :], vec[:, V_B_DT:V_B_DT + 2], -SOFTPLUS_KNEE, 0.1, ALU.add, ALU.mult)
            dve.wait_ge(prep_mm, 2)
            nc.vector.tensor_copy(gates[:, :, :, :], bank[6].rearrange("p (a h n) -> p a h n", a=2, h=2)).then_inc(prep, 1)
            dve.wait_ge(prep_mm, 3)
            nc.vector.tensor_copy(centred_bias[:, :], bank[7][:, 0:2]).then_inc(prep, 1)
            dve.wait_ge(made, 1)

            def total(b, slot):
                for h in range(HALVES):
                    dve.wait_ge(dt_ln, b * 2 + h + 1)
                    stt(out=decay_s[:, b, h], in0=along(bank[2 * slot + h]), scalar=knee[:, h:h + 1],
                        in1=along(acc[4 + 2 * slot + h]), op0=ALU.max, op1=ALU.add).then_inc(dt_sum, 1)

            def unit_b(b, slot, previous):
                for h in range(HALVES):
                    dve.wait_ge(dt_ready, b * 2 + h + 1)
                    dve.wait_ge(dt_sum, b * 2 + h + 1)
                    ts(acc[4 + 2 * slot + h], bank[2 * slot + h], vec[:, V_B_DT + h:V_B_DT + h + 1], SOFTPLUS_KNEE,
                       ALU.add, ALU.min).then_inc(dt_capped, 1)
                if previous:
                    total(b - 1, 1 - slot)

            sequences(dve, unit_b, total)

            ts(one_minus_mu[:, :], vec[:, V_MU_R:V_MU_R + 2], -1.0, 1.0, ALU.mult, ALU.add)
            ts(minus_bq[:, :], vec[:, V_BQ:V_BQ + 1], -1.0, None, ALU.mult)
            nc.vector.reciprocal(inv_scale[:, :], sc[:, 0:1])
            eight = w[:, W_CENTRED + 3 * P:W_CENTRED + 4 * P]
            four = w[:, W_CENTRED:W_CENTRED + 4 * P].rearrange("p (a n) -> p a n", a=4)
            chain = (
                lambda: tt(both_scales[:, :], sc[:, 0:1], sc[:, 1:2], ALU.mult),
                lambda: ts(eight, eight, both_scales[:, 0:1], None, ALU.mult),
                lambda: nc.vector.tensor_reduce(row_sum[:, :], four, AXIS_X, ALU.add),
                lambda: ts(row_sum[:, :], row_sum[:, :], -1.0 / CHANNELS, None, ALU.mult),
                lambda: tt(four, four, row_sum[:, :].unsqueeze(2).broadcast_to([P, 4, P]), ALU.add),
                lambda: nc.vector.tensor_copy(w8[:, 0, :], eight),
                lambda: tt(w8_rest[:, :], eight, w8[:, 0, :], ALU.subtract),
                lambda: nc.vector.tensor_copy(w8[:, 1, :], w8_rest[:, :]),
                lambda: tt(w8_rest[:, :], w8_rest[:, :], w8[:, 1, :], ALU.subtract),
            )
            for n, make in enumerate(chain):
                make().then_inc(made, 1)
                dve.wait_ge(made, n + 2)
            nc.vector.tensor_copy(w8[:, 2, :], w8_rest[:, :]).then_inc(prep, 1)

            def gate_input(c):
                dve.wait_ge(alpha_done, 2 * c + 2)
                dve.wait_ge(gate_done, RING + 2 * c + 1)
                for h in reversed(range(HALVES)):
                    if h == 0:
                        dve.wait_ge(gated_step, 2 * c + 1)
                    stt(out=state[:, c, h, :], in0=decay[:, c, h, :], scalar=-1.0, in1=state[:, c, 0, :],
                        op0=ALU.add, op1=ALU.mult).then_inc(gated_step, 1)
                dve.wait_ge(gated_step, 2 * c + 2)
                ts(decay[:, c], decay[:, c], 0.01, 0.99, ALU.max, ALU.min)
                tt(state[:, c], state[:, c], xconv[:, c], ALU.mult).then_inc(gated_done, 1)

            def scan(c):
                segments = [t_[:, c, :, :].rearrange("p h (b l) -> p h b l", b=SEQS) for t_ in (decay, state)]
                first_a, first_g = (t_[:, :, :, 0] for t_ in segments)
                dve.wait_ge(gated_done, c + 1)
                if c:
                    dve.wait_ge(carry_done, c)
                    tt(entering[:, :, :], first_a, carried[:, :, :], ALU.mult).then_inc(entering_done, 1)
                    dve.wait_ge(entering_done, c)
                    tt(first_g, first_g, entering[:, :, :], ALU.subtract)
                nc.vector.memset(first_a, 0.0).then_inc(edge_done, 1)
                flat = state[:, c, :, :].rearrange("p h n -> p (h n)")
                dve.wait_ge(edge_done, c + 1)
                nc.vector.tensor_tensor_scan(flat, decay[:, c, :, :].rearrange("p h n -> p (h n)"), flat, 0.0,
                                             ALU.mult, ALU.subtract).then_inc(scan_done, 1)

            def carry(c):
                g = state[:, c, :, :]
                dve.wait_ge(scan_done, c + 1)
                nc.vector.tensor_copy(carried[:, :, :], g.rearrange("p h (b l) -> p h b l", b=SEQS)[:, :, :, SPAN - 1]
                                      ).then_inc(carry_done, 1)
                dve.wait_ge(carry_done, c + 1)
                dve.wait_ge(gate_done, RING + 2 * c + 2)
                tt(g, g, c_gate[:, c, :].unsqueeze(1).broadcast_to([P, HALVES, CHUNK]), ALU.mult).then_inc(cgated, 1)

            def skip(c):
                dve.wait_ge(cgated, c + 1)
                for h in range(HALVES):
                    g = state[:, c, h, :]
                    last = stt(out=g, in0=xconv[:, c, h, :], scalar=vec[:, V_D + h:V_D + h + 1], in1=g,
                               op0=ALU.mult, op1=ALU.add)
                last.then_inc(skip_done, 1)

            def gate_z(c):
                dve.wait_ge(skip_done, c + 1)
                g = state[:, c, :, :]
                tt(g, g, silu_z[:, c, :, :], ALU.mult).then_inc(y_done, 1)

            def norm1(c):
                dve.wait_ge(rstd_done[0], c + 1)
                tt(x1[c], bank[OUT_BANK], rstd[c], ALU.mult).then_inc(x1_done, 1)

            MAGIC = 1.5 * 2.0 ** 20

            def round_a(c):
                dve.wait_ge(xs_done, c + 1)
                ts(step8[c].bitcast(I32), xs[c].bitcast(I32), 0x7F800000, None, ALU.bitwise_and).then_inc(quant_step, 1)

            def round_b(c):
                dve.wait_ge(quant_step, 4 * c + 1)
                ts(step8[c], step8[c], 2.0 ** -6, 2.0 ** 8, ALU.max, ALU.min).then_inc(quant_step, 1)

            def round_c(c):
                dve.wait_ge(quant_step, 4 * c + 2)
                stt(out=xs[c], in0=step8[c], scalar=MAGIC, in1=xs[c], op0=ALU.mult, op1=ALU.add).then_inc(quant_step, 1)

            def round_d(c):
                dve.wait_ge(quant_step, 4 * c + 3)
                stt(out=quant[c], in0=step8[c], scalar=-MAGIC, in1=xs[c], op0=ALU.mult, op1=ALU.add).then_inc(quant_step, 1)

            def round_e(c):
                dve.wait_ge(quant_step, 4 * c + 4)
                ts(quant[c], quant[c], FP8_MAX, -FP8_MAX, ALU.min, ALU.max).then_inc(quant_done, 1)

            def sum2(c):
                dve.wait_ge(ffn_ready, c + 1)
                stt(out=x2[c], in0=bank[FFN_BANK], scalar=centred_bias[:, 0:1], in1=x1[c],
                    op0=ALU.add, op1=ALU.add).then_inc(y2_done, 1)

            def norm2(c):
                dve.wait_ge(rstd_done[1], c + 1)
                tt(x2[c], x2[c], rstd[c], ALU.mult).then_inc(x2_done, 1)

            def logits(c):
                dve.wait_ge(score_ready, c + 1)
                tt(grouped(prob[c]), grouped(bank[SCORE_BANK]), mask_all_groups, ALU.max).then_inc(logit_done, 1)

            def row_least(c):
                dve.wait_ge(logit_done, c + 1)
                nc.vector.tensor_reduce(least[:, c, :], grouped(prob[c]), AXIS_X, ALU.min).then_inc(least_done, 1)

            def normalise(c):
                dve.wait_ge(exp_done, c + 1)
                nc.vector.reciprocal(inv_sum[:, c, :], exp_sum[:, c, :]).then_inc(inv_done, 1)
                dve.wait_ge(inv_done, c + 1)
                p = grouped(prob[c])
                tt(p, p, inv_sum[:, c, :].unsqueeze(2).broadcast_to([P, GROUPS, P]), ALU.mult).then_inc(prob_done, 1)

            def sum3(c):
                dve.wait_ge(att_ready, c + 1)
                stt(out=y3[c], in0=bank[ATT_BANK], scalar=centred_bias[:, 1:2], in1=x2[c],
                    op0=ALU.add, op1=ALU.add).then_inc(y3_done, 1)

            def norm3(c):
                dve.wait_ge(rstd_done[2], c + 1)
                tt(x_groups[:, c], by_position(y3[c]), by_position(rstd[c]), ALU.mult).then_inc(x3_done, 1)

            whole = xT[:, :].rearrange("p (b l) -> p b l", b=SEQS)

            def difference(c):
                dve.wait_ge(x3_done, c + 1)
                d = in_chunk(x_diff[c])
                at, skip_first = c * SPAN, int(c == 0)
                last = tt(d[:, :, skip_first:], whole[:, :, at + skip_first - 1:at + SPAN - 1],
                          whole[:, :, at + skip_first:at + SPAN], ALU.subtract)
                if skip_first:
                    last = ts(d[:, :, 0:1], whole[:, :, 0:1], -1.0, None, ALU.mult)
                last.then_inc(diff_done, 1)

            def mix_k(c):
                dve.wait_ge(diff_done, c + 1)
                stt(out=in_chunk(xk[c]), in0=in_chunk(x_diff[c]), scalar=one_minus_mu[:, 1:2], in1=x_chunks[:, c],
                    op0=ALU.mult, op1=ALU.add).then_inc(xk_done, 1)

            def mix_r(c):
                dve.wait_ge(diff_done, c + 1)
                stt(out=in_chunk(xr[c]), in0=in_chunk(x_diff[c]), scalar=one_minus_mu[:, 0:1], in1=x_chunks[:, c],
                    op0=ALU.mult, op1=ALU.add).then_inc(xr_done, 1)

            def gate_values(c):
                dve.wait_ge(r_done, c + 1)
                dve.wait_ge(fv_ready, c + 1)
                tt(y4[c], bank[FV_BANK], r[c], ALU.mult).then_inc(rv_done, 1)

            def sum4(c):
                dve.wait_ge(rv_done, c + 1)
                tt(in_chunk(y4[c]), in_chunk(y4[c]), x_chunks[:, c], ALU.add).then_inc(y4_done, 1)

            def norm4(c):
                dve.wait_ge(rstd_done[3], c + 1)
                tt(result[c], bank[CEN_BANK], rstd[c], ALU.mult).then_inc(out_done, 1)

            pipeline((5, gate_z), (9, norm3), (8, logits), (8, row_least), (9, difference), (6, round_a), (9, mix_k),
                     (6, round_b), (7, norm2), (8, normalise), (9, mix_r), (6, round_c), (4, scan), (6, round_d),
                     (8, sum3), (0, gate_input), (6, round_e), (10, norm4), (4, carry), (9, gate_values), (6, sum2),
                     (4, skip), (9, sum4), (5, norm1))


def kernel(**inputs):
    import numpy as np
    import concourse.bacc as bacc
    from concourse.bass_utils import run_bass_kernel_spmd

    a = {k: np.asarray(v) for k, v in inputs.items()}

    def halves(m):
        return m.reshape(HALVES, P, -1).transpose(1, 0, 2).reshape(P, -1)

    weights = np.concatenate([
        halves(a["L0_attn_W_x"][2 * STATE:]), halves(a["L0_attn_W_dt"].T), halves(a["L0_attn_W_out"].T),
        a["L1_attn_Wv"].T, a["L0_ffn_weight_fp8"].T, a["L1_attn_Wq"].T, a["L1_attn_Wk"].T,
        a["L1_ffn_W_r"].T, a["L1_ffn_W_k"].T, a["L1_ffn_W_v"].T], axis=1)
    columns = [halves(a["L0_attn_conv_w"].reshape(INNER, TAPS))]
    columns += [halves(a[n].reshape(INNER, 1)) for n in ("L0_attn_conv_b", "L0_attn_b_dt", "L0_attn_D")]
    columns += [a[n].reshape(P, 1) for n in ("L0_ffn_bias", "L1_attn_bv", "L1_attn_bq", "L1_attn_bk",
                                             "L1_ffn_mu_r", "L1_ffn_mu_k")]
    position = np.arange(P) % GROUP
    same = position[:, None] == position[None, :]
    eye = np.eye(P, dtype=np.float32)
    constants = np.concatenate([eye, eye - np.float32(1.0 / CHANNELS),
                                np.where(same, 0.0, MASKED).astype(np.float32)], axis=1)
    arrays = {
        "x_t": a["L0_attn_x"].reshape(TOKENS, CHANNELS).T,
        "w_in_t": a["L0_attn_W_in"].T,
        "vectors": np.concatenate(columns, axis=1),
        "weights": weights,
        "gate_rows": a["L0_attn_W_x"][:2 * STATE].reshape(2, STATE, INNER).transpose(1, 0, 2),
        "scales": np.concatenate([a["L0_ffn_input_scale"], a["L0_ffn_weight_scale"]]),
        "constants": constants,
    }
    arrays = {k: np.ascontiguousarray(v) for k, v in arrays.items()}
    nc = bacc.Bacc("TRN2", target_bir_lowering=False, num_devices=1)
    args = [nc.dram_tensor(k, v.shape, mybir.dt.from_np(v.dtype), kind="ExternalInput").ap() for k, v in arrays.items()]
    args.append(nc.dram_tensor("out_t", (CHANNELS, TOKENS), F32, kind="ExternalOutput").ap())
    build(nc, *args)
    r = run_bass_kernel_spmd(nc, [arrays], core_ids=[0])
    out = r.results[0]["out_t"].reshape(CHANNELS, CHUNKS, SEQS, SPAN)
    return np.ascontiguousarray(out.transpose(2, 1, 3, 0)).reshape(SEQS, LENGTH, CHANNELS)
```

```python
from contextlib import ExitStack

import concourse.bass as bass
from concourse import mybir

ALU = mybir.AluOpType
ACT = mybir.ActivationFunctionType
AXIS_X = mybir.AxisListType.X
F32 = mybir.dt.float32
BF16 = mybir.dt.bfloat16
I32 = mybir.dt.int32

P = 128
SEQS, LENGTH, CHANNELS = 8, 512, 128
TOKENS = SEQS * LENGTH
HALVES = 2
INNER = HALVES * P
TAPS = 4
STATE = 16
CHUNK = 512
SPAN = CHUNK // SEQS
GROUP = P // SEQS
GROUPS = CHUNK // P
CHUNKS = TOKENS // CHUNK
EPS = 1e-5
FP8_MAX = 448.0
MASKED = 1e30

W_COMB_X = 0
W_COMB_DT = W_COMB_X + HALVES * INNER
W_CENTRED = W_COMB_DT + HALVES * INNER
W_Q = W_CENTRED + 4 * P
W_K = W_Q + P
W_FR = W_K + P
W_FK = W_FR + P
W_FV = W_FK + P
W_COLS = W_FV + P
V_CONV_W = 0
V_CONV_B = V_CONV_W + HALVES * TAPS
V_B_DT = V_CONV_B + HALVES
V_D = V_B_DT + HALVES
V_BIAS8 = V_D + HALVES
V_BV = V_BIAS8 + 1
V_BQ = V_BV + 1
V_BK = V_BQ + 1
V_MU_R = V_BK + 1
V_MU_K = V_MU_R + 1
V_COLS = V_MU_K + 1
C_IDENT = 0
C_CENTRE = P
C_MASK = 2 * P
C_COLS = 3 * P


def build(nc, x_t, w_in_t, vectors, weights, gate_rows, scales, constants, out_t):
    with ExitStack() as ctx:
        def sb(name, shape, dt=F32):
            return ctx.enter_context(nc.sbuf_tensor(name, shape, dt))

        def sem(name):
            return ctx.enter_context(nc.semaphore(name))

        xT = sb("xT", [P, TOKENS])
        xconv = sb("xconv", [P, CHUNKS, HALVES, CHUNK])
        silu_z = sb("silu_z", [P, CHUNKS, HALVES, CHUNK])
        decay = sb("decay", [P, CHUNKS, HALVES, CHUNK])
        state = sb("state", [P, CHUNKS, HALVES, CHUNK])
        c_gate = sb("c_gate", [P, CHUNKS, CHUNK])

        w_in = sb("w_in", [P, 2 * INNER])
        vec = sb("vec", [P, V_COLS])
        w = sb("w", [P, W_COLS])
        gate_w = sb("gate_w", [STATE, 2, INNER])
        sc = sb("sc", [P, 2])
        const = sb("const", [P, C_COLS])
        comb = sb("comb", [P, HALVES, INNER])
        gates = sb("gates", [P, 2, HALVES, P])
        w8 = sb("w8", [P, 3, P], BF16)
        w8_rest = sb("w8_rest", [P, P])
        sixteenth = sb("sixteenth", [STATE, P])
        mean_w = sb("mean_w", [P, P])
        half_w = sb("half_w", [P, P])
        row_sum = sb("row_sum", [P, 4])
        both_scales = sb("both_scales", [P, 1])
        inv_scale = sb("inv_scale", [P, 1])
        minus_b_dt = sb("minus_b_dt", [P, HALVES])
        alpha_bias = sb("alpha_bias", [P, HALVES])
        one_minus_mu = sb("one_minus_mu", [P, 2])
        minus_bq = sb("minus_bq", [P, 1])
        centred_bias = sb("centred_bias", [P, 2])
        eps = sb("eps", [P, 1])
        credit = sb("credit", [P, 16])
        carried = sb("carried", [P, HALVES, SEQS])
        entering = sb("entering", [P, HALVES, SEQS])
        least = sb("least", [P, CHUNKS, GROUPS])
        exp_sum = sb("exp_sum", [P, CHUNKS, GROUPS])
        inv_sum = sb("inv_sum", [P, CHUNKS, GROUPS])

        ident = const[:, C_IDENT:C_IDENT + P]
        centre = const[:, C_CENTRE:C_CENTRE + P]
        mask = const[:, C_MASK:C_MASK + P]
        mask_all_groups = mask.unsqueeze(1).broadcast_to([P, GROUPS, P])

        def by_sequence(array):
            return array[:, :, :, :].rearrange("p c h (b l) -> p b h c l", b=SEQS)

        xconv_s, silu_z_s = by_sequence(xconv), by_sequence(silu_z)

        def along(ap):
            return ap.rearrange("p (c l) -> p c l", c=CHUNKS)

        y_groups = state[:, :, :, :].rearrange("p c h (b g l) -> p c h g b l", b=SEQS, g=GROUPS)
        x_groups = xT[:, :].rearrange("p (b c g l) -> p c g b l", b=SEQS, c=CHUNKS, g=GROUPS)
        x_chunks = xT[:, :].rearrange("p (b c l) -> p c b l", b=SEQS, c=CHUNKS)

        def grouped(ap):
            return ap.rearrange("p (g n) -> p g n", g=GROUPS)

        def by_position(ap):
            return ap.rearrange("p (g b l) -> p g b l", g=GROUPS, b=SEQS)

        def in_chunk(ap):
            return ap.rearrange("p (b l) -> p b l", b=SEQS)

        def tiles(array, half):
            return [array[:, c, half, :] for c in range(CHUNKS)]

        x1 = prob = xk = tiles(xconv, 0)
        xs = v = k_act = tiles(xconv, 1)
        step8 = k_ = k_relu = tiles(decay, 0)
        quant = [t.bitcast(BF16)[:, 0:CHUNK] for t in tiles(decay, 1)]
        k_sq = xr = tiles(decay, 1)
        sq = x_diff = tiles(silu_z, 0)
        rstd = tiles(silu_z, 1)
        x2 = result = [c_gate[:, c, :] for c in range(CHUNKS)]
        q = prob_t = r = tiles(state, 0)
        q_sq = y3 = y4 = tiles(state, 1)

        psum = ctx.enter_context(nc.psum_tensor("psum", [P, 8, CHUNK], F32))
        bank = [psum[:, n, :] for n in range(8)]
        OUT_BANK = 0
        VAR_BANK = 1
        CEN_BANK = 2
        K_BANK = SCORE_BANK = 3
        Q_BANK = FR_BANK = 4
        TURN_BANK = 5
        FFN_BANK = FV_BANK = ATT_BANK = 6
        V_BANK = FK_BANK = 7

        x_first, x_next, x_rest, small_in, z_in, weights_in = (
            sem(n) for n in ("x_first", "x_next", "x_rest", "small_in", "z_in", "weights_in"))
        filled = sem("filled")
        prep_mm, prep, made = sem("prep_mm"), sem("prep"), sem("made")
        xp_ready, z_ready, tap_done, conv_step, conv_done, xconv_done, z_done = (
            sem(n) for n in ("xp_ready", "z_ready", "tap_done", "conv_step", "conv_done", "xconv_done", "z_done"))
        dt_ready, dt_abs, dt_exp, dt_ln, dt_sum = (sem(n) for n in ("dt_ready", "dt_abs", "dt_exp", "dt_ln", "dt_sum"))
        gate_ready, gate_done, alpha_done, gated_step, gated_done = (
            sem(n) for n in ("gate_ready", "gate_done", "alpha_done", "gated_step", "gated_done"))
        entering_done, edge_done, scan_done, carry_done, cgated, skip_done, y_done = (
            sem(n) for n in ("entering_done", "edge_done", "scan_done", "carry_done", "cgated", "skip_done", "y_done"))
        out_ready, x1_done, xs_done, quant_step, quant_done = (
            sem(n) for n in ("out_ready", "x1_done", "xs_done", "quant_step", "quant_done"))
        sq_done, var_ready, var_read, rstd_done = (
            [sem(f"{n}{m + 1}") for m in range(4)] for n in ("sq_done", "var_ready", "var_read", "rstd_done"))
        ffn_ready, y2_done, x2_done = sem("ffn_ready"), sem("y2_done"), sem("x2_done")
        q_ready, k_ready, v_ready, q_done, k_done, v_done = (
            sem(n) for n in ("q_ready", "k_ready", "v_ready", "q_done", "k_done", "v_done"))
        score_ready, logit_done, least_done, exp_done, inv_done, prob_done = (
            sem(n) for n in ("score_ready", "logit_done", "least_done", "exp_done", "inv_done", "prob_done"))
        turned_ready, turned_done, att_ready, y3_done, x3_done = (
            sem(n) for n in ("turned_ready", "turned_done", "att_ready", "y3_done", "x3_done"))
        diff_done, xk_done, xr_done, fk_ready, relu_done, kact_done = (
            sem(n) for n in ("diff_done", "xk_done", "xr_done", "fk_ready", "relu_done", "kact_done"))
        fr_ready, r_exp, r_ln, r_done, fv_ready, rv_done, y4_done, cen_ready, out_done, stored = (
            sem(n) for n in ("fr_ready", "r_exp", "r_ln", "r_done", "fv_ready", "rv_done", "y4_done", "cen_ready",
                             "out_done", "stored"))

        RING = 4
        FIRST_PART = 5
        FIRST = SEQS // 2

        block = ctx.enter_context(nc.Block())

        def in_turn(eng, count, unit, last):
            unit(0, 0, False)
            with eng.Fori(0, count // 2 - 1) as i:
                unit(i * 2 + 1, 1, True)
                unit(i * 2 + 2, 0, True)
            unit(count - 1, 1, True)
            last(count - 1, 1)

        EARLY = CHUNKS // 2
        DT_BANKS = [4, 6, 0, 2] + [4, 6] * 2
        GATE_BANKS = DT_BANKS[:EARLY] + [0, 2] * 2

        def pipeline(late, *work):
            turns = [(first + every * c, n, c) for n, (first, every, stage) in enumerate(work)
                     for c in range(EARLY if stage in late else 0, CHUNKS)]
            for _, n, c in sorted(turns):
                work[n][2](c)

        @block.sync
        def _(sp):
            sp.dma_start(w_in[:, 0:INNER], w_in_t[:, 0:INNER]).then_inc(small_in, 16)
            sp.dma_start(w_in[:, INNER:], w_in_t[:, INNER:]).then_inc(z_in, 16)
            sp.dma_start(xT[:, LENGTH:FIRST * LENGTH], x_t[:, LENGTH:FIRST * LENGTH]).then_inc(x_next, 16)
            sp.dma_start(xT[:, FIRST * LENGTH:], x_t[:, FIRST * LENGTH:]).then_inc(x_rest, 16)
            sp.dma_start(w[:, :], weights).then_inc(weights_in, 16)
            sp.dma_start(const[:, :], constants).then_inc(weights_in, 16)
            sp.dma_start(gate_w[:, :, :], gate_rows).then_inc(weights_in, 16)
            sp.dma_start(sc[:, :], scales.rearrange("(a n) -> a n", a=1).broadcast_to([P, 2])).then_inc(weights_in, 16)
            with sp.Fori(0, CHUNKS // 2) as i:
                for k in range(2):
                    c = i * 2 + k
                    sp.wait_ge(out_done, c + 1)
                    sp.dma_start(out_t[:, bass.ts(c, CHUNK)], c_gate[:, c, :]).then_inc(stored, 16)
            sp.wait_ge(stored, 16 * CHUNKS)

        @block.tensor
        def _(pe):
            def mm(out, lhs_t, rhs, first=True, last=True, open_group=False):
                return nc.tensor.matmul(out, lhs_t, rhs, start=first, stop=last, skip_group_check=open_group)

            def project(i, first_pair=False, weights_made=False):
                for slot in range(2):
                    b = i * 2 + slot
                    if first_pair and slot == 1:
                        pe.wait_ge(x_next, 16)
                    for h in range(HALVES):
                        k = 2 * slot + h
                        pe.wait_ge(conv_done, i * 4 + k + 1)
                        mm(bank[k], w_in[:, h * P:(h + 1) * P], xT[:, bass.ts(b, CHUNK)]).then_inc(xp_ready, 1)
                    if first_pair and slot == 0:
                        pe.wait_ge(z_in, 16)
                    if weights_made:
                        pe.wait_ge(prep, 3)
                    for h in range(HALVES):
                        k = 2 * slot + h
                        pe.wait_ge(z_done, i * 4 + k + 1)
                        mm(bank[4 + k], w_in[:, INNER + h * P:INNER + (h + 1) * P],
                           xT[:, bass.ts(b, CHUNK)]).then_inc(z_ready, 1)

            pe.wait_ge(small_in, 32)
            pe.wait_ge(x_first, 16)
            pe.wait_ge(filled, 1)
            for i in range(FIRST // 2):
                project(i, first_pair=i == 0)

            pe.wait_ge(weights_in, 64)
            pe.wait_ge(z_done, RING + 2 * FIRST)
            for ih in range(HALVES):
                for mh in range(HALVES):
                    last = mm(bank[4 + ih][:, 0:INNER],
                              w[:, W_COMB_X + mh * INNER + ih * P:W_COMB_X + mh * INNER + (ih + 1) * P],
                              w[:, W_COMB_DT + mh * INNER:W_COMB_DT + (mh + 1) * INNER], mh == 0, mh == 1)
            last.then_inc(prep_mm, 1)
            for gate in range(2):
                for ih in range(HALVES):
                    last = mm(bank[6][:, (2 * gate + ih) * P:(2 * gate + ih + 1) * P],
                              gate_w[:, gate, ih * P:(ih + 1) * P], sixteenth[:, :])
            last.then_inc(prep_mm, 1)
            mm(bank[7][:, 0:2], centre, vec[:, V_BIAS8:V_BIAS8 + 2]).then_inc(prep_mm, 1)

            pe.wait_ge(x_rest, 16)
            with pe.Fori(FIRST // 2, SEQS // 2) as i:
                project(i, weights_made=True)

            def dt_product(c, seqs, signal=True):
                cols = slice(seqs.start * SPAN, seqs.stop * SPAN)
                for h in range(HALVES):
                    for ih in range(HALVES):
                        last = mm(bank[DT_BANKS[c] + h][:, cols], comb[:, ih, h * P:(h + 1) * P], xconv[:, c, ih, cols], ih == 0, ih == 1)
                    if signal:
                        last.then_inc(dt_ready, 1)

            def gate_means(c):
                for gate in range(2):
                    for ih in range(HALVES):
                        last = mm(bank[GATE_BANKS[c] + gate], gates[:, gate, ih, :], xconv[:, c, ih, :], ih == 0, ih == 1)
                    last.then_inc(gate_ready, 1)

            pe.wait_ge(xconv_done, RING + 2 * FIRST_PART)
            for c in range(2):
                pe.wait_ge(z_done, RING + 2 * (SEQS - 1 + c))
                dt_product(c, range(FIRST_PART), signal=False)
            pe.wait_ge(xconv_done, RING + 2 * SEQS)
            for c in range(2):
                dt_product(c, range(FIRST_PART, SEQS))
            for c in range(2, EARLY):
                dt_product(c, range(SEQS))

            for c in range(EARLY):
                pe.wait_ge(dt_sum, 2 * c + 2)
                gate_means(c)

            free = [None] * 8
            for c in range(EARLY):
                at = GATE_BANKS[c]
                free[at:at + 2] = [(gate_done, 2 * c + 2)] * 2

            def dt_late(c):
                at = DT_BANKS[c]
                pe.wait_ge(*free[at])
                pe.wait_ge(*free[at + 1])
                dt_product(c, range(SEQS))
                free[at:at + 2] = [(dt_sum, 2 * c + 2)] * 2

            def gates_late(c):
                at = GATE_BANKS[c]
                pe.wait_ge(*free[at])
                pe.wait_ge(*free[at + 1])
                gate_means(c)
                free[at:at + 2] = [(gate_done, 2 * c + 2)] * 2

            def out_proj(c):
                pe.wait_ge(y_done, c + 1)
                pe.wait_ge(*free[OUT_BANK])
                for h in range(HALVES):
                    mm(by_position(bank[OUT_BANK]), w[:, W_CENTRED + h * P:W_CENTRED + (h + 1) * P], y_groups[:, c, h], h == 0, False)
                mm(by_position(bank[OUT_BANK]), centre, x_groups[:, c], False, True).then_inc(out_ready, 1)
                free[OUT_BANK] = (x1_done, c + 1)

            def variance(n):
                def of(c):
                    pe.wait_ge(sq_done[n], c + 1)
                    pe.wait_ge(*free[VAR_BANK])
                    mm(bank[VAR_BANK], mean_w[:, :], sq[c]).then_inc(var_ready[n], 1)
                    free[VAR_BANK] = (var_read[n], c + 1)
                return of

            var1, var2, var3, var4 = (variance(n) for n in range(4))

            def ffn(c):
                pe.wait_ge(quant_done, c + 1)
                pe.wait_ge(*free[FFN_BANK])
                for part in range(3):
                    last = mm(bank[FFN_BANK], w8[:, part, :], quant[c], part == 0, part == 2)
                last.then_inc(ffn_ready, 1)
                free[FFN_BANK] = (y2_done, c + 1)

            def queries(c):
                pe.wait_ge(x2_done, c + 1)
                pe.wait_ge(*free[Q_BANK])
                mm(bank[Q_BANK], w[:, W_Q:W_Q + P], x2[c]).then_inc(q_ready, 1)
                free[Q_BANK] = (q_done, c + 1)

            def keys(c):
                pe.wait_ge(x2_done, c + 1)
                pe.wait_ge(*free[K_BANK])
                mm(bank[K_BANK], w[:, W_K:W_K + P], x2[c]).then_inc(k_ready, 1)
                free[K_BANK] = (k_done, c + 1)

            def values(c):
                pe.wait_ge(x2_done, c + 1)
                pe.wait_ge(*free[V_BANK])
                for g in range(GROUPS):
                    cols = slice(g * P, (g + 1) * P)
                    last = mm(bank[V_BANK][:, cols], x2[c][:, cols], w[:, W_CENTRED + 2 * P:W_CENTRED + 3 * P])
                last.then_inc(v_ready, 1)
                free[V_BANK] = (v_done, c + 1)

            def scores(c):
                s = bank[SCORE_BANK]
                pe.wait_ge(q_done, c + 1)
                pe.wait_ge(k_done, c + 1)
                pe.wait_ge(*free[SCORE_BANK])
                mm(s, half_w[:, :], k_sq[c], True, False, True)
                for g in range(GROUPS):
                    cols = slice(g * P, (g + 1) * P)
                    mm(s[:, cols], q_sq[c][:, cols], half_w[:, :], False, False, True)
                    last = mm(s[:, cols], q[c][:, cols], k_[c][:, cols], False, True, True)
                last.then_inc(score_ready, 1)
                free[SCORE_BANK] = (logit_done, c + 1)

            def turn(c):
                pe.wait_ge(prob_done, c + 1)
                pe.wait_ge(*free[TURN_BANK])
                for g in range(GROUPS):
                    cols = slice(g * P, (g + 1) * P)
                    last = nc.tensor.transpose(bank[TURN_BANK][:, cols], prob[c][:, cols], ident)
                last.then_inc(turned_ready, 1)
                free[TURN_BANK] = (turned_done, c + 1)

            def attend(c):
                pe.wait_ge(turned_done, c + 1)
                pe.wait_ge(v_done, c + 1)
                pe.wait_ge(*free[ATT_BANK])
                for g in range(GROUPS):
                    cols = slice(g * P, (g + 1) * P)
                    last = mm(bank[ATT_BANK][:, cols], v[c][:, cols], prob_t[c][:, cols])
                last.then_inc(att_ready, 1)
                free[ATT_BANK] = (y3_done, c + 1)

            def mix_keys(c):
                pe.wait_ge(xk_done, c + 1)
                pe.wait_ge(*free[FK_BANK])
                mm(bank[FK_BANK], w[:, W_FK:W_FK + P], xk[c]).then_inc(fk_ready, 1)
                free[FK_BANK] = (relu_done, c + 1)

            def mix_gate(c):
                pe.wait_ge(xr_done, c + 1)
                pe.wait_ge(*free[FR_BANK])
                mm(bank[FR_BANK], w[:, W_FR:W_FR + P], xr[c]).then_inc(fr_ready, 1)
                free[FR_BANK] = (r_exp, c + 1)

            def mix_values(c):
                pe.wait_ge(kact_done, c + 1)
                pe.wait_ge(*free[FV_BANK])
                mm(bank[FV_BANK], w[:, W_FV:W_FV + P], k_act[c]).then_inc(fv_ready, 1)
                free[FV_BANK] = (rv_done, c + 1)

            def centre4(c):
                pe.wait_ge(y4_done, c + 1)
                pe.wait_ge(*free[CEN_BANK])
                mm(bank[CEN_BANK], centre, y4[c]).then_inc(cen_ready, 1)
                free[CEN_BANK] = (out_done, c + 1)

            pe.wait_ge(prep, 4)
            pipeline((dt_late, gates_late),
                     (-317542, 34526, dt_late), (-180371, 31945, gates_late), (13267, 32009, out_proj),
                     (35966, 31754, var1), (68144, 31057, ffn), (69638, 31986, var2), (83059, 32151, queries),
                     (89999, 31013, keys), (100533, 31945, scores), (94086, 34493, values), (129648, 31131, turn),
                     (135423, 32031, attend), (150769, 32074, var3), (183995, 31664, mix_keys),
                     (195612, 31731, mix_gate), (210583, 31927, mix_values), (228375, 31441, centre4),
                     (237989, 32892, var4))

        @block.scalar
        def _(act):
            act.dma_start(xT[:, 0:LENGTH], x_t[:, 0:LENGTH]).then_inc(x_first, 16)
            act.dma_start(vec[:, :], vectors).then_inc(small_in, 16)
            acc = [state[:, n // 2, n % 2, :] for n in range(8)]

            nc.scalar.preload_act_table(ACT.Silu)
            act.wait_ge(small_in, 32)

            def conv_silu(b, slot):
                for h in range(HALVES):
                    act.wait_ge(conv_done, RING + b * 2 + h + 1)
                    nc.scalar.activation(xconv_s[:, b, h], along(acc[2 * slot + h]), ACT.Silu).then_inc(xconv_done, 1)

            def unit_a(b, slot, previous):
                for h in range(HALVES):
                    j, k = b * 2 + h, 2 * slot + h
                    act.wait_ge(xp_ready, j + 1)
                    act.wait_ge(xconv_done, j + 1)
                    nc.scalar.activation(acc[k], bank[k], ACT.Identity,
                                         bias=vec[:, V_CONV_B + h:V_CONV_B + h + 1],
                                         scale=vec[:, V_CONV_W + h * TAPS + 3:V_CONV_W + h * TAPS + 4]).then_inc(tap_done, 1)
                for h in range(HALVES):
                    j, k = b * 2 + h, 2 * slot + h
                    act.wait_ge(z_ready, j + 1)
                    nc.scalar.activation(silu_z_s[:, b, h], along(bank[4 + k]), ACT.Silu).then_inc(z_done, 1)
                if previous:
                    conv_silu(b - 1, 1 - slot)

            in_turn(act, SEQS, unit_a, conv_silu)

            def log_exp(c):
                for h in range(HALVES):
                    act.wait_ge(dt_ready, c * 2 + h + 1)
                    nc.scalar.activation(state[:, c, h, :], bank[DT_BANKS[c] + h], ACT.Abs,
                                         bias=vec[:, V_B_DT + h:V_B_DT + h + 1]).then_inc(dt_abs, 1)
                for h in range(HALVES):
                    act.wait_ge(dt_abs, c * 2 + h + 1)
                    nc.scalar.activation(state[:, c, h, :], state[:, c, h, :], ACT.Exp, scale=-1.0).then_inc(dt_exp, 1)
                for h in range(HALVES):
                    act.wait_ge(dt_exp, c * 2 + h + 1)
                    nc.scalar.activation(state[:, c, h, :], state[:, c, h, :], ACT.Ln, bias=1.0).then_inc(dt_ln, 1)

            def sigmoids(c):
                for h in range(HALVES):
                    act.wait_ge(dt_sum, c * 2 + h + 1)
                    a = decay[:, c, h, :]
                    nc.scalar.activation(a, a, ACT.Sigmoid, bias=alpha_bias[:, h:h + 1], scale=0.1).then_inc(alpha_done, 1)
                act.wait_ge(gate_ready, c * 2 + 1)
                nc.scalar.activation(state[:, c, 0, :], bank[GATE_BANKS[c]], ACT.Sigmoid).then_inc(gate_done, 1)
                act.wait_ge(gate_ready, c * 2 + 2)
                nc.scalar.activation(c_gate[:, c, :], bank[GATE_BANKS[c] + 1], ACT.Sigmoid).then_inc(gate_done, 1)

            nc.scalar.preload_act_table_set("natural_log_exp_and_others")
            act.wait_ge(xconv_done, RING + 2 * SEQS)
            for c in range(EARLY):
                log_exp(c)
            nc.scalar.preload_act_table(ACT.Sigmoid)
            for c in range(EARLY):
                sigmoids(c)

            nc.scalar.preload_act_table_set("natural_log_exp_and_others")

            def sigmoids_late(c):
                if c == EARLY:
                    nc.scalar.preload_act_table(ACT.Sigmoid)
                sigmoids(c)
                if c == CHUNKS - 1:
                    nc.scalar.preload_act_table_set("natural_log_exp_and_others")

            def square(n):
                def of(c):
                    source, ready = ((bank[OUT_BANK], out_ready), (x2[c], y2_done), (y3[c], y3_done),
                                     (bank[CEN_BANK], cen_ready))[n]
                    act.wait_ge(ready, c + 1)
                    nc.scalar.activation(sq[c], source, ACT.Square).then_inc(sq_done[n], 1)
                return of

            def inv_std(n):
                def of(c):
                    act.wait_ge(var_ready[n], c + 1)
                    nc.scalar.activation(rstd[c], bank[VAR_BANK], ACT.Ln, bias=eps[:, 0:1]).then_inc(var_read[n], 1)
                    act.wait_ge(var_read[n], c + 1)
                    nc.scalar.activation(rstd[c], rstd[c], ACT.Exp, scale=-0.5).then_inc(rstd_done[n], 1)
                return of

            square1, square2, square3, square4 = (square(n) for n in range(4))
            inv_std1, inv_std2, inv_std3, inv_std4 = (inv_std(n) for n in range(4))

            def rescale(c):
                act.wait_ge(x1_done, c + 1)
                nc.scalar.activation(xs[c], x1[c], ACT.Identity, scale=inv_scale[:, 0:1]).then_inc(xs_done, 1)

            def keep_queries(c):
                act.wait_ge(q_ready, c + 1)
                nc.scalar.activation(q[c], bank[Q_BANK], ACT.Identity, bias=minus_bq[:, 0:1], scale=-1.0)
                nc.scalar.activation(q_sq[c], bank[Q_BANK], ACT.Square, bias=vec[:, V_BQ:V_BQ + 1]).then_inc(q_done, 1)

            def keep_keys(c):
                act.wait_ge(k_ready, c + 1)
                nc.scalar.activation(k_[c], bank[K_BANK], ACT.Identity, bias=vec[:, V_BK:V_BK + 1])
                nc.scalar.activation(k_sq[c], bank[K_BANK], ACT.Square, bias=vec[:, V_BK:V_BK + 1]).then_inc(k_done, 1)

            def keep_values(c):
                act.wait_ge(v_ready, c + 1)
                nc.scalar.activation(v[c], bank[V_BANK], ACT.Copy).then_inc(v_done, 1)

            def softmax_exp(c):
                act.wait_ge(least_done, c + 1)
                for g in range(GROUPS):
                    cols = slice(g * P, (g + 1) * P)
                    e = nc.scalar.activation(prob[c][:, cols], prob[c][:, cols], ACT.Exp, bias=least[:, c, g:g + 1],
                                             scale=-1.0, accum_out=exp_sum[:, c, g:g + 1])
                e.then_inc(exp_done, 1)

            def normalise(c):
                act.wait_ge(inv_done, c + 1)
                for g in range(GROUPS):
                    cols = slice(g * P, (g + 1) * P)
                    last = nc.scalar.activation(prob[c][:, cols], prob[c][:, cols], ACT.Identity, scale=inv_sum[:, c, g:g + 1])
                last.then_inc(prob_done, 1)

            def keep_turned(c):
                act.wait_ge(turned_ready, c + 1)
                nc.scalar.activation(prob_t[c], bank[TURN_BANK], ACT.Copy).then_inc(turned_done, 1)

            def relu_squared(c):
                act.wait_ge(fk_ready, c + 1)
                nc.scalar.activation(k_relu[c], bank[FK_BANK], ACT.Relu).then_inc(relu_done, 1)
                act.wait_ge(relu_done, c + 1)
                nc.scalar.activation(k_act[c], k_relu[c], ACT.Square).then_inc(kact_done, 1)

            def gate_sigmoid(c):
                act.wait_ge(fr_ready, c + 1)
                nc.scalar.activation(r[c], bank[FR_BANK], ACT.Exp, scale=-1.0).then_inc(r_exp, 1)
                act.wait_ge(r_exp, c + 1)
                nc.scalar.activation(r[c], r[c], ACT.Ln, bias=1.0).then_inc(r_ln, 1)
                act.wait_ge(r_ln, c + 1)
                nc.scalar.activation(r[c], r[c], ACT.Exp, scale=-1.0).then_inc(r_done, 1)

            pipeline((log_exp, sigmoids_late),
                     (-618459, 31754, log_exp), (-153471, 32815, sigmoids_late), (45049, 33533, square1),
                     (63201, 31931, inv_std1), (70329, 31818, rescale), (99799, 31672, square2),
                     (102887, 31825, inv_std2), (122234, 31581, keep_queries), (126744, 31377, keep_keys),
                     (137914, 31408, softmax_exp), (132787, 33214, keep_values), (146629, 32758, normalise),
                     (161758, 31462, keep_turned), (172949, 32792, square3), (181862, 34022, inv_std3),
                     (222110, 31931, relu_squared), (228778, 32225, gate_sigmoid), (261520, 31889, square4),
                     (278486, 31589, inv_std4))

        @block.vector
        def _(dve):
            tt, ts, stt = nc.vector.tensor_tensor, nc.vector.tensor_scalar, nc.vector.scalar_tensor_tensor
            acc = [state[:, n // 2, n % 2, :] for n in range(8)]

            nc.vector.memset(sixteenth[:, :], 1.0 / STATE)
            nc.vector.memset(mean_w[:, :], 1.0 / CHANNELS)
            nc.vector.memset(half_w[:, :], 0.5)
            nc.vector.memset(eps[:, :], EPS).then_inc(filled, 1)
            for at, ring in enumerate((conv_done, z_done, xconv_done)):
                nc.vector.memset(credit[:, at:at + 1], 0.0).then_inc(ring, RING)

            dve.wait_ge(small_in, 32)

            def convolve(i):
                for slot in range(2):
                    for tap in (2, 1, 0):
                        shift = TAPS - 1 - tap
                        for h in range(HALVES):
                            k = 2 * slot + h
                            if tap == 2:
                                dve.wait_ge(tap_done, i * 4 + k + 1)
                            else:
                                dve.wait_ge(conv_step, i * 8 + 4 * slot + 2 * (1 - tap) + h + 1)
                            part = acc[k][:, shift:]
                            col = V_CONV_W + h * TAPS + tap
                            done = stt(out=part, in0=bank[k][:, 0:CHUNK - shift], scalar=vec[:, col:col + 1], in1=part,
                                       op0=ALU.mult, op1=ALU.add)
                            done.then_inc(conv_done if tap == 0 else conv_step, 1)

            with dve.Fori(0, FIRST // 2) as i:
                convolve(i)

            dve.wait_ge(weights_in, 64)
            dve.wait_ge(prep_mm, 1)
            nc.vector.tensor_copy(comb[:, :, :], psum[:, 4:6, 0:INNER]).then_inc(prep, 1)
            ts(minus_b_dt[:, :], vec[:, V_B_DT:V_B_DT + 2], -1.0, None, ALU.mult).then_inc(made, 1)
            ts(alpha_bias[:, :], vec[:, V_B_DT:V_B_DT + 2], 0.1, None, ALU.mult)
            dve.wait_ge(prep_mm, 2)
            nc.vector.tensor_copy(gates[:, :, :, :], bank[6].rearrange("p (a h n) -> p a h n", a=2, h=2)).then_inc(prep, 1)
            dve.wait_ge(prep_mm, 3)
            nc.vector.tensor_copy(centred_bias[:, :], bank[7][:, 0:2]).then_inc(prep, 1)
            dve.wait_ge(made, 1)

            with dve.Fori(FIRST // 2, SEQS // 2) as i:
                convolve(i)

            ts(one_minus_mu[:, :], vec[:, V_MU_R:V_MU_R + 2], -1.0, 1.0, ALU.mult, ALU.add)
            ts(minus_bq[:, :], vec[:, V_BQ:V_BQ + 1], -1.0, None, ALU.mult)
            nc.vector.reciprocal(inv_scale[:, :], sc[:, 0:1])
            eight = w[:, W_CENTRED + 3 * P:W_CENTRED + 4 * P]
            four = w[:, W_CENTRED:W_CENTRED + 4 * P].rearrange("p (a n) -> p a n", a=4)
            chain = (
                lambda: tt(both_scales[:, :], sc[:, 0:1], sc[:, 1:2], ALU.mult),
                lambda: ts(eight, eight, both_scales[:, 0:1], None, ALU.mult),
                lambda: nc.vector.tensor_reduce(row_sum[:, :], four, AXIS_X, ALU.add),
                lambda: ts(row_sum[:, :], row_sum[:, :], -1.0 / CHANNELS, None, ALU.mult),
                lambda: tt(four, four, row_sum[:, :].unsqueeze(2).broadcast_to([P, 4, P]), ALU.add),
                lambda: nc.vector.tensor_copy(w8[:, 0, :], eight),
                lambda: tt(w8_rest[:, :], eight, w8[:, 0, :], ALU.subtract),
                lambda: nc.vector.tensor_copy(w8[:, 1, :], w8_rest[:, :]),
                lambda: tt(w8_rest[:, :], w8_rest[:, :], w8[:, 1, :], ALU.subtract),
            )
            for n, make in enumerate(chain):
                make().then_inc(made, 1)
                dve.wait_ge(made, n + 2)
            nc.vector.tensor_copy(w8[:, 2, :], w8_rest[:, :]).then_inc(prep, 1)

            def total(c, h):
                dve.wait_ge(dt_ln, c * 2 + h + 1)
                stt(out=decay[:, c, h, :], in0=bank[DT_BANKS[c] + h], scalar=minus_b_dt[:, h:h + 1], in1=state[:, c, h, :],
                    op0=ALU.max, op1=ALU.add).then_inc(dt_sum, 1)

            for c in range(EARLY):
                for h in range(HALVES):
                    total(c, h)

            def total_late(c):
                for h in range(HALVES):
                    total(c, h)

            def gate_input(c):
                dve.wait_ge(alpha_done, 2 * c + 2)
                dve.wait_ge(gate_done, 2 * c + 1)
                for h in reversed(range(HALVES)):
                    if h == 0:
                        dve.wait_ge(gated_step, 2 * c + 1)
                    stt(out=state[:, c, h, :], in0=decay[:, c, h, :], scalar=-1.0, in1=state[:, c, 0, :],
                        op0=ALU.add, op1=ALU.mult).then_inc(gated_step, 1)
                dve.wait_ge(gated_step, 2 * c + 2)
                ts(decay[:, c], decay[:, c], 0.01, 0.99, ALU.max, ALU.min)
                tt(state[:, c], state[:, c], xconv[:, c], ALU.mult).then_inc(gated_done, 1)

            def scan(c):
                segments = [t_[:, c, :, :].rearrange("p h (b l) -> p h b l", b=SEQS) for t_ in (decay, state)]
                first_a, first_g = (t_[:, :, :, 0] for t_ in segments)
                dve.wait_ge(gated_done, c + 1)
                if c:
                    dve.wait_ge(carry_done, c)
                    tt(entering[:, :, :], first_a, carried[:, :, :], ALU.mult).then_inc(entering_done, 1)
                    dve.wait_ge(entering_done, c)
                    tt(first_g, first_g, entering[:, :, :], ALU.subtract)
                nc.vector.memset(first_a, 0.0).then_inc(edge_done, 1)
                flat = state[:, c, :, :].rearrange("p h n -> p (h n)")
                dve.wait_ge(edge_done, c + 1)
                nc.vector.tensor_tensor_scan(flat, decay[:, c, :, :].rearrange("p h n -> p (h n)"), flat, 0.0,
                                             ALU.mult, ALU.subtract).then_inc(scan_done, 1)

            def carry(c):
                g = state[:, c, :, :]
                dve.wait_ge(scan_done, c + 1)
                nc.vector.tensor_copy(carried[:, :, :], g.rearrange("p h (b l) -> p h b l", b=SEQS)[:, :, :, SPAN - 1]
                                      ).then_inc(carry_done, 1)
                dve.wait_ge(carry_done, c + 1)
                dve.wait_ge(gate_done, 2 * c + 2)
                tt(g, g, c_gate[:, c, :].unsqueeze(1).broadcast_to([P, HALVES, CHUNK]), ALU.mult).then_inc(cgated, 1)

            def skip(c):
                dve.wait_ge(cgated, c + 1)
                for h in range(HALVES):
                    g = state[:, c, h, :]
                    last = stt(out=g, in0=xconv[:, c, h, :], scalar=vec[:, V_D + h:V_D + h + 1], in1=g,
                               op0=ALU.mult, op1=ALU.add)
                last.then_inc(skip_done, 1)

            def gate_z(c):
                dve.wait_ge(skip_done, c + 1)
                g = state[:, c, :, :]
                tt(g, g, silu_z[:, c, :, :], ALU.mult).then_inc(y_done, 1)

            def norm1(c):
                dve.wait_ge(rstd_done[0], c + 1)
                tt(x1[c], bank[OUT_BANK], rstd[c], ALU.mult).then_inc(x1_done, 1)

            MAGIC = 1.5 * 2.0 ** 20

            def round_a(c):
                dve.wait_ge(xs_done, c + 1)
                ts(step8[c].bitcast(I32), xs[c].bitcast(I32), 0x7F800000, None, ALU.bitwise_and).then_inc(quant_step, 1)

            def round_b(c):
                dve.wait_ge(quant_step, 4 * c + 1)
                ts(step8[c], step8[c], 2.0 ** -6, 2.0 ** 8, ALU.max, ALU.min).then_inc(quant_step, 1)

            def round_c(c):
                dve.wait_ge(quant_step, 4 * c + 2)
                stt(out=xs[c], in0=step8[c], scalar=MAGIC, in1=xs[c], op0=ALU.mult, op1=ALU.add).then_inc(quant_step, 1)

            def round_d(c):
                dve.wait_ge(quant_step, 4 * c + 3)
                stt(out=quant[c], in0=step8[c], scalar=-MAGIC, in1=xs[c], op0=ALU.mult, op1=ALU.add).then_inc(quant_step, 1)

            def round_e(c):
                dve.wait_ge(quant_step, 4 * c + 4)
                ts(quant[c], quant[c], FP8_MAX, -FP8_MAX, ALU.min, ALU.max).then_inc(quant_done, 1)

            def sum2(c):
                dve.wait_ge(ffn_ready, c + 1)
                stt(out=x2[c], in0=bank[FFN_BANK], scalar=centred_bias[:, 0:1], in1=x1[c],
                    op0=ALU.add, op1=ALU.add).then_inc(y2_done, 1)

            def norm2(c):
                dve.wait_ge(rstd_done[1], c + 1)
                tt(x2[c], x2[c], rstd[c], ALU.mult).then_inc(x2_done, 1)

            def logits(c):
                dve.wait_ge(score_ready, c + 1)
                tt(grouped(prob[c]), grouped(bank[SCORE_BANK]), mask_all_groups, ALU.max).then_inc(logit_done, 1)

            def row_least(c):
                dve.wait_ge(logit_done, c + 1)
                nc.vector.tensor_reduce(least[:, c, :], grouped(prob[c]), AXIS_X, ALU.min).then_inc(least_done, 1)

            def inv_sums(c):
                dve.wait_ge(exp_done, c + 1)
                nc.vector.reciprocal(inv_sum[:, c, :], exp_sum[:, c, :]).then_inc(inv_done, 1)

            def sum3(c):
                dve.wait_ge(att_ready, c + 1)
                stt(out=y3[c], in0=bank[ATT_BANK], scalar=centred_bias[:, 1:2], in1=x2[c],
                    op0=ALU.add, op1=ALU.add).then_inc(y3_done, 1)

            def norm3(c):
                dve.wait_ge(rstd_done[2], c + 1)
                tt(x_groups[:, c], by_position(y3[c]), by_position(rstd[c]), ALU.mult).then_inc(x3_done, 1)

            whole = xT[:, :].rearrange("p (b l) -> p b l", b=SEQS)

            def difference(c):
                dve.wait_ge(x3_done, c + 1)
                d = in_chunk(x_diff[c])
                at, skip_first = c * SPAN, int(c == 0)
                last = tt(d[:, :, skip_first:], whole[:, :, at + skip_first - 1:at + SPAN - 1],
                          whole[:, :, at + skip_first:at + SPAN], ALU.subtract)
                if skip_first:
                    last = ts(d[:, :, 0:1], whole[:, :, 0:1], -1.0, None, ALU.mult)
                last.then_inc(diff_done, 1)

            def mix_k(c):
                dve.wait_ge(diff_done, c + 1)
                stt(out=in_chunk(xk[c]), in0=in_chunk(x_diff[c]), scalar=one_minus_mu[:, 1:2], in1=x_chunks[:, c],
                    op0=ALU.mult, op1=ALU.add).then_inc(xk_done, 1)

            def mix_r(c):
                dve.wait_ge(diff_done, c + 1)
                stt(out=in_chunk(xr[c]), in0=in_chunk(x_diff[c]), scalar=one_minus_mu[:, 0:1], in1=x_chunks[:, c],
                    op0=ALU.mult, op1=ALU.add).then_inc(xr_done, 1)

            def gate_values(c):
                dve.wait_ge(r_done, c + 1)
                dve.wait_ge(fv_ready, c + 1)
                tt(y4[c], bank[FV_BANK], r[c], ALU.mult).then_inc(rv_done, 1)

            def sum4(c):
                dve.wait_ge(rv_done, c + 1)
                tt(in_chunk(y4[c]), in_chunk(y4[c]), x_chunks[:, c], ALU.add).then_inc(y4_done, 1)

            def norm4(c):
                dve.wait_ge(rstd_done[3], c + 1)
                tt(result[c], bank[CEN_BANK], rstd[c], ALU.mult).then_inc(out_done, 1)

            pipeline((total_late,),
                     (-7064, 15011, total_late), (4424, 24144, gate_input), (30153, 31730, scan), (44652, 33578, carry),
                     (86433, 32734, skip), (97697, 31707, gate_z), (126085, 32073, norm1), (131797, 31672, round_a),
                     (133888, 32767, round_b), (135370, 33924, round_c), (145886, 32432, round_d),
                     (149961, 32025, round_e), (153664, 32191, sum2), (168079, 32093, norm2), (193476, 31931, logits),
                     (197597, 31617, row_least), (205977, 31889, inv_sums), (230641, 31788, sum3),
                     (255859, 31851, norm3), (270324, 31701, difference), (271827, 31990, mix_k), (279250, 32064, mix_r),
                     (307940, 31377, gate_values), (308452, 31557, sum4), (344225, 31353, norm4))


def kernel(**inputs):
    import numpy as np
    import concourse.bacc as bacc
    from concourse.bass_utils import run_bass_kernel_spmd

    a = {k: np.asarray(v) for k, v in inputs.items()}

    def halves(m):
        return m.reshape(HALVES, P, -1).transpose(1, 0, 2).reshape(P, -1)

    weights = np.concatenate([
        halves(a["L0_attn_W_x"][2 * STATE:]), halves(a["L0_attn_W_dt"].T), halves(a["L0_attn_W_out"].T),
        a["L1_attn_Wv"].T, a["L0_ffn_weight_fp8"].T, a["L1_attn_Wq"].T, a["L1_attn_Wk"].T,
        a["L1_ffn_W_r"].T, a["L1_ffn_W_k"].T, a["L1_ffn_W_v"].T], axis=1)
    columns = [halves(a["L0_attn_conv_w"].reshape(INNER, TAPS))]
    columns += [halves(a[n].reshape(INNER, 1)) for n in ("L0_attn_conv_b", "L0_attn_b_dt", "L0_attn_D")]
    columns += [a[n].reshape(P, 1) for n in ("L0_ffn_bias", "L1_attn_bv", "L1_attn_bq", "L1_attn_bk",
                                             "L1_ffn_mu_r", "L1_ffn_mu_k")]
    position = np.arange(P) % GROUP
    same = position[:, None] == position[None, :]
    eye = np.eye(P, dtype=np.float32)
    constants = np.concatenate([eye, eye - np.float32(1.0 / CHANNELS),
                                np.where(same, 0.0, MASKED).astype(np.float32)], axis=1)
    arrays = {
        "x_t": a["L0_attn_x"].reshape(TOKENS, CHANNELS).T,
        "w_in_t": a["L0_attn_W_in"].T,
        "vectors": np.concatenate(columns, axis=1),
        "weights": weights,
        "gate_rows": a["L0_attn_W_x"][:2 * STATE].reshape(2, STATE, INNER).transpose(1, 0, 2),
        "scales": np.concatenate([a["L0_ffn_input_scale"], a["L0_ffn_weight_scale"]]),
        "constants": constants,
    }
    arrays = {k: np.ascontiguousarray(v) for k, v in arrays.items()}
    nc = bacc.Bacc("TRN2", target_bir_lowering=False, num_devices=1)
    args = [nc.dram_tensor(k, v.shape, mybir.dt.from_np(v.dtype), kind="ExternalInput").ap() for k, v in arrays.items()]
    args.append(nc.dram_tensor("out_t", (CHANNELS, TOKENS), F32, kind="ExternalOutput").ap())
    build(nc, *args)
    r = run_bass_kernel_spmd(nc, [arrays], core_ids=[0])
    out = r.results[0]["out_t"].reshape(CHANNELS, CHUNKS, SEQS, SPAN)
    return np.ascontiguousarray(out.transpose(2, 1, 3, 0)).reshape(SEQS, LENGTH, CHANNELS)
```
